# Optimizing a Trainium2 kernel written in Bass

```python
import numpy as np
import jax
import jax.numpy as jnp

def _softmax(x, axis=-1):
    return jax.nn.softmax(x, axis=axis)

def _gelu(x):
    return jax.nn.gelu(x, approximate=True)

def _silu(x):
    return jax.nn.silu(x)

def _sigmoid(x):
    return jax.nn.sigmoid(x)

def _layernorm(x, axis=-1, eps=1e-05):
    m = jnp.mean(x, axis=axis, keepdims=True)
    v = jnp.var(x, axis=axis, keepdims=True)
    return (x - m) / jnp.sqrt(v + eps)

def _scatter_add(tgt, idx, src, axis=0):
    return tgt.at[idx].add(src)

def _segment_sum(src, seg, n):
    return jax.ops.segment_sum(src, seg, n)
kernel_name = 'mk_gnn_resnorm_d1_gnn_r64_b60282'

def setup_inputs(seed: int=0):
    np.random.seed(seed)
    _w = jnp.asarray

    def _rec_inputs():
        import jax
        import jax.numpy as jnp
        _gk = jax.random.key(seed)
        x = -0.0002117 + 1 * jax.random.normal(jax.random.fold_in(_gk, 1), (100000, 256), jnp.float32)
        src = jax.random.randint(jax.random.fold_in(_gk, 2), (25000,), 0, 100000, jnp.int32)
        dst = jax.random.randint(jax.random.fold_in(_gk, 3), (25000,), 0, 100000, jnp.int32)
        _o = jnp.argsort(dst, stable=True)
        src = src[_o]
        dst = dst[_o]
        edge_weight = jax.random.uniform(jax.random.fold_in(_gk, 12), (25000,), jnp.float32, 0.0, 0.03125)
        return (x, src, dst, edge_weight)
    x, src, dst, edge_weight = _rec_inputs()

    def _L0_gnn_setup():
        import jax, jax.numpy as jnp
        import numpy as np
        N_NODES = 100000
        N_EDGES = 50000
        D_IN = 256
        N_BLOCKS = 4
        D_OUT = 256

        def _spmm(edge_src, edge_dst, edge_weight, feats, n_nodes):
            msgs = edge_weight[:, None] * feats[edge_src]
            return jax.ops.segment_sum(msgs, edge_dst, num_segments=n_nodes)
        key = jax.random.key(seed)
        ks = jax.random.split(key, 6)
        x = jax.random.normal(ks[0], (N_NODES, D_IN), dtype=jnp.float32)
        edge_src = jax.random.randint(ks[1], (N_EDGES,), 0, N_NODES, dtype=jnp.int32)
        edge_dst = jax.random.randint(ks[2], (N_EDGES,), 0, N_NODES, dtype=jnp.int32)
        edge_weight = jax.random.uniform(ks[3], (N_EDGES,), dtype=jnp.float32) / 32.0
        stdv_w = 1.0 / np.sqrt(D_OUT)
        shared_weight = jax.random.uniform(ks[4], (D_IN * N_BLOCKS, D_OUT), minval=-stdv_w, maxval=stdv_w, dtype=jnp.float32)
        stdv_b = 1.0 / np.sqrt(D_OUT)
        output_bias = jax.random.uniform(ks[5], (D_OUT,), minval=-stdv_b, maxval=stdv_b, dtype=jnp.float32)
        return {'x': x, 'edge_src': edge_src, 'edge_dst': edge_dst, 'edge_weight': edge_weight, 'shared_weight': shared_weight, 'output_bias': output_bias}
    _L0_gnn_all = _L0_gnn_setup()
    _L0_gnn_in = {k: v for k, v in _L0_gnn_all.items() if k in ('shared_weight', 'output_bias')}
    del _L0_gnn_all
    return {'x': x, 'src': src, 'dst': dst, 'edge_weight': edge_weight, 'L0_gnn_shared_weight': _L0_gnn_in['shared_weight'], 'L0_gnn_output_bias': _L0_gnn_in['output_bias']}

def reference(x, src, dst, edge_weight, L0_gnn_shared_weight, L0_gnn_output_bias):
    import jax
    import jax.numpy as jnp

    def _L0_gnn_ref(x, edge_src, edge_dst, edge_weight, shared_weight, output_bias):
        import jax, jax.numpy as jnp
        import numpy as np
        N_NODES = 100000
        N_EDGES = 50000
        D_IN = 256
        N_BLOCKS = 4
        D_OUT = 256

        def _spmm(edge_src, edge_dst, edge_weight, feats, n_nodes):
            msgs = edge_weight[:, None] * feats[edge_src]
            return jax.ops.segment_sum(msgs, edge_dst, num_segments=n_nodes)
        n_nodes, d_in = x.shape
        n_blocks = shared_weight.shape[0] // d_in
        feats = [x]
        cur = x
        for _ in range(n_blocks - 1):
            cur = _spmm(edge_src, edge_dst, edge_weight, cur, n_nodes)
            feats.append(cur)
        concat = jnp.concatenate(feats, axis=1)
        return concat @ shared_weight + output_bias
    x = _layernorm(x + _L0_gnn_ref(x, src, dst, edge_weight, L0_gnn_shared_weight, L0_gnn_output_bias), axis=-1)
    return x

_drawn_inputs = setup_inputs


def setup_inputs(seed=0):
    import zlib

    import numpy as np

    out = dict(_drawn_inputs(seed))
    spreads = {}
    factors = {'edge_weight': 25.137}
    for name, (base, spread) in spreads.items():
        noise = np.random.default_rng([zlib.crc32(name.encode()), seed]).standard_normal(out[name].shape)
        drawn = base * np.exp(spread * noise) if base else spread * noise
        out[name] = jnp.asarray(drawn.astype(out[name].dtype))
    for name, factor in factors.items():
        out[name] = (out[name] * factor).astype(out[name].dtype)
    return out
```

```python
def gnn_program(nc, x, src, dst, edge_weight, weight, bias, out):
    import concourse.bass as bass
    from concourse import mybir
    from contextlib import ExitStack

    f32, i32 = mybir.dt.float32, mybir.dt.int32
    ALU = mybir.AluOpType
    ACT = mybir.ActivationFunctionType

    N, D = x.shape
    E = src.shape[0]
    P = 128
    KC = D // P
    BLOCKS = weight.shape[0] // D
    EPS = 1e-5

    RPP = 4
    UROWS = P * RPP
    UNITS = N // UROWS
    TAIL_ROWS = N - UNITS * UROWS
    TAIL_RPP = 2
    TAIL_P = TAIL_ROWS // TAIL_RPP
    assert TAIL_P * TAIL_RPP == TAIL_ROWS and TAIL_P % 16 == 0
    RING = 3
    BODIES = UNITS // RING
    assert BODIES * RING == UNITS

    EPT = P - 1
    G = 4
    TILES = -(-E // EPT)
    TILES += -TILES % (2 * G)
    GROUPS = TILES // G
    FULL = E // EPT
    REST = E - FULL * EPT
    SLOTS = 2 * P
    assert 0 < REST < EPT and P < FULL < SLOTS - 1 and TILES <= SLOTS
    A_BODIES = GROUPS
    B_BODIES = BODIES - A_BODIES
    B_REST = GROUPS - RING * B_BODIES
    assert B_BODIES > 0 and B_REST >= 0
    TABLE_OPS = TILES // (GROUPS // 2)
    HALF = GROUPS // 2
    ABSENT = 1 << 23
    CROWS = TILES * P
    TABLE_COLS = -(-N // P)

    c_dram = [nc.dram_tensor(f"c{n}_rows", (CROWS, D), f32).ap() for n in (1, 2)]
    tail_of_node = nc.dram_tensor("tail_of_node", (TABLE_COLS * P, 1), i32).ap()
    keys_out_dram = nc.dram_tensor("keys_out", (SLOTS * P,), f32).ap()

    ctx = ExitStack()
    with ctx:
        def sb(name, shape, dt=f32):
            return ctx.enter_context(nc.sbuf_tensor(name, shape, dt))

        def pb(name):
            return ctx.enter_context(nc.psum_tensor(name, [P, 2 * D], f32))

        def sem(name):
            return ctx.enter_context(nc.semaphore(name))

        def sems(name, n):
            return [sem(f"{name}{k}") for k in range(n)]

        ident = sb("ident", [P, P])
        w_sb = sb("w_sb", [P, BLOCKS * KC, D])
        bias2 = sb("bias2", [P, 2 * D])
        eps = sb("eps", [P, 1])
        x_ring = [sb(f"x_ring{k}", [P, RPP * D]) for k in range(RING)]
        xT = [sb(f"xT{k}", [P, 2 * D]) for k in range(2)]
        y_ring = [sb(f"y_ring{k}", [P, RPP * D]) for k in range(RING)]
        o_ring = [sb(f"o_ring{k}", [P, RPP * D]) for k in range(RING)]
        stats = [sb(f"stats{k}", [P, RPP, 6]) for k in range(RING)]
        mean_var = [sb(f"mean_var{k}", [P, RPP, 2]) for k in range(RING)]
        std = [sb(f"std{k}", [P, RPP]) for k in range(RING)]
        rstd = [sb(f"rstd{k}", [P, RPP]) for k in range(RING)]
        shift = [sb(f"shift{k}", [P, RPP]) for k in range(RING)]
        rows_in = [sb(f"rows_in{k}", [P, D]) for k in range(G)]
        sums = [sb(f"sums{k}", [P, G, D]) for k in range(RING)]
        sel = [sb(f"sel{k}", [P, P]) for k in range(G)]
        keys_out = sb("keys_out_bc", [P, TILES * P])
        dst_i = sb("dst_i", [P, 2, P], i32)
        next_i = sb("next_i", [P, 2, P], i32)
        src_i = sb("src_i", [P, 2, P], i32)
        w_l = sb("w_l", [P, 2, P])
        dst_f = sb("dst_f", [P, 2, P])
        next_f = sb("next_f", [P, 2, P])
        src_f = sb("src_f", [P, 2, P])
        keys_f = sb("keys_f", [P, 2, P])
        key_in = sb("key_in", [P, SLOTS])
        w1 = sb("w1", [P, SLOTS])
        w2 = sb("w2", [P, SLOTS])
        src_node = sb("src_node", [P, SLOTS], i32)
        tail_node = sb("tail_node", [P, SLOTS], i32)
        tail_f = sb("tail_f", [P, SLOTS])
        row_number = sb("row_number", [P, SLOTS], i32)
        src_tail = sb("src_tail", [P, SLOTS], i32)
        absent = sb("absent", [P, TABLE_COLS], i32)
        gather_idx = [sb(f"gather_idx{k}", [P, G], i32) for k in range(RING)]
        tailx_idx = [sb(f"tailx_idx{k}", [P, G], i32) for k in range(2)]
        tailo_idx = [sb(f"tailo_idx{k}", [P, G], i32) for k in range(2)]
        table_idx = sb("table_idx", [P, TABLE_OPS], i32)
        table_val = sb("table_val", [P, TABLE_OPS], i32)
        found = sb("found", [P, TABLE_OPS], i32)
        tail_x = [x_ring[0][:, k * D:(k + 1) * D] for k in range(G)]
        c1_in = [x_ring[1][:, k * D:(k + 1) * D] for k in range(G)]
        c2_in = [x_ring[2][:, k * D:(k + 1) * D] for k in range(G)]
        catT = y_ring[0:2]
        cy = [y_ring[2][:, k * D:(k + 1) * D] for k in range(G)]
        co = [o_ring[0][:, k * D:(k + 1) * D] for k in range(G)]
        cstats = [sb(f"cstats{k}", [P, 6]) for k in range(G)]
        cmv = [sb(f"cmv{k}", [P, 2]) for k in range(G)]
        cstd = [sb(f"cstd{k}", [P, 1]) for k in range(G)]
        crstd = [sb(f"crstd{k}", [P, 1]) for k in range(G)]
        cshift = [sb(f"cshift{k}", [P, 1]) for k in range(G)]

        ps_xT = [pb(f"ps_xT{k}") for k in range(2)]
        ps_y = [pb(f"ps_y{k}") for k in range(2)]
        ps_sum = [pb(f"ps_sum{k}") for k in range(2)]

        blank = sem("blank")
        consts = sem("consts")
        edges_loaded = sem("edges_loaded")
        weights_loaded = sem("weights_loaded")
        identity_ready = sem("identity_ready")
        w0_ready = sem("w0_ready")
        floats_ready = sem("floats_ready")
        keys_stored = sem("keys_stored")
        keys_loaded = sem("keys_loaded")
        lists_turned = sem("lists_turned")
        table_chain = sem("table_chain")
        tables_ready = sem("tables_ready")
        numbers_ready = sem("numbers_ready")
        table_blank = sem("table_blank")
        x_loaded = sems("x_loaded", RING)
        xT_psum = sem("xT_psum")
        xT_copied = sem("xT_copied")
        y_psum = sem("y_psum")
        y_copied = sem("y_copied")
        stats_ready = sem("stats_ready")
        var_ready = sem("var_ready")
        std_ready = sem("std_ready")
        rstd_ready = sem("rstd_ready")
        shift_ready = sem("shift_ready")
        normed = sem("normed")
        stored = sems("stored", RING)
        gather_staged = sem("gather_staged")
        gathered = sems("gathered", G)
        sel_ready = sem("sel_ready")
        carry_ready = sem("carry_ready")
        summed = sem("summed")
        sum_copied = sem("sum_copied")
        sums_stored = sems("sums_stored", RING)
        table_staged = sem("table_staged")
        table_done = sem("table_done")
        found_copied = sem("found_copied")
        w2_ready = sem("w2_ready")
        tailo_staged = sem("tailo_staged")
        tailx_in = sems("tailx_in", G)
        c1_loaded = sems("c1_loaded", G)
        c2_loaded = sems("c2_loaded", G)
        ta_psum = sem("ta_psum")
        ta_copied = sem("ta_copied")
        tb_psum = sem("tb_psum")
        tb_copied = sem("tb_copied")
        cy_psum = sem("cy_psum")
        cy_copied = sem("cy_copied")
        cstats_ready = sem("cstats_ready")
        cvar_ready = sem("cvar_ready")
        cstd_ready = sem("cstd_ready")
        crstd_ready = sem("crstd_ready")
        cshift_ready = sem("cshift_ready")
        cnormed = sem("cnormed")
        scattered = sems("scattered", G)

        ctx.enter_context(nc.allow_non_contiguous_dma(reason="a few hundred single keys and four-byte table entries"))
        block = ctx.enter_context(nc.Block())

        A_STORES = [GROUPS * (k == 0) for k in range(RING)]
        ALL_STORES = [A_STORES[k] + len(range(k, GROUPS, RING)) for k in range(RING)]

        def until(eng, s, value):
            if not isinstance(value, int) or value > 0:
                eng.wait_ge(s, value)

        PAIRS = 2 * UNITS + 1

        def unit_rows(ap, u):
            return ap[bass.ds(u * UROWS, UROWS), :].rearrange("(p r) d -> p (r d)", r=RPP)

        tail_rows = [ap[UNITS * UROWS:N, :].rearrange("(p r) d -> p (r d)", r=TAIL_RPP) for ap in (x, out)]

        @block.sync
        def _(sp):
            def as_column(ap):
                return ap.rearrange("(t o) -> t o", o=1)

            sp.dma_start(w_sb[:, :, :], weight.rearrange("(c p) n -> p c n", p=P)).then_inc(weights_loaded, 16)
            for k in range(2):
                sp.dma_start(bias2[:, k * D:(k + 1) * D], bias.partition_broadcast(P)).then_inc(weights_loaded, 16)
            for u in range(RING):
                sp.dma_start(x_ring[u][:, :], unit_rows(x, u)).then_inc(x_loaded[u], 16)
            sp.wait_ge(blank, 5)
            for table, ap in ((dst_i, dst), (src_i, src), (w_l, edge_weight)):
                whole = ap[0:FULL * EPT].rearrange("(t c) -> t c", c=EPT)
                sp.dma_start(table[:, 0, 1:P], whole[0:P, :]).then_inc(edges_loaded, 16)
                sp.dma_start(table[0:FULL - P, 1, 1:P], whole[P:FULL, :]).then_inc(edges_loaded, 16)
                sp.dma_start(table[FULL - P:FULL - P + 1, 1, 1:1 + REST],
                             ap[FULL * EPT:E].rearrange("(o c) -> o c", o=1)).then_inc(edges_loaded, 16)
            whole = dst[0:FULL * EPT].rearrange("(t c) -> t c", c=EPT)
            sp.dma_start(dst_i[1:P, 0, 0:1], whole[0:P - 1, EPT - 1:EPT]).then_inc(edges_loaded, 16)
            sp.dma_start(dst_i[0:FULL - P + 1, 1, 0:1], whole[P - 1:FULL, EPT - 1:EPT]).then_inc(edges_loaded, 16)
            sp.dma_start(next_i[:, 0, 0:EPT], whole[0:P, :]).then_inc(edges_loaded, 16)
            sp.dma_start(next_i[0:FULL - P, 1, 0:EPT], whole[P:FULL, :]).then_inc(edges_loaded, 16)
            sp.dma_start(next_i[FULL - P:FULL - P + 1, 1, 0:REST],
                         dst[FULL * EPT:E].rearrange("(o c) -> o c", o=1)).then_inc(edges_loaded, 16)
            sp.dma_start(next_i[:, 0, EPT:P], whole[1:P + 1, 0:1]).then_inc(edges_loaded, 16)
            sp.dma_start(next_i[0:FULL - P - 1, 1, EPT:P], whole[P + 1:FULL, 0:1]).then_inc(edges_loaded, 16)
            sp.dma_start(next_i[FULL - P - 1:FULL - P, 1, EPT:P],
                         as_column(dst[FULL * EPT:FULL * EPT + 1])).then_inc(edges_loaded, 16)
            sp.dma_start(tail_of_node.rearrange("(p c) o -> p (c o)", p=P), absent[:, :]).then_inc(table_blank, 16)
            sp.wait_ge(floats_ready, 4)
            sp.dma_start(keys_out_dram.rearrange("(h p c) -> p h c", h=2, c=P), keys_f[:, :, :]).then_inc(keys_stored, 16)
            sp.wait_ge(keys_stored, 16)
            sp.dma_start(keys_out[:, :], keys_out_dram[0:TILES * P].partition_broadcast(P)).then_inc(keys_loaded, 16)

            def load_unit(u, k):
                sp.wait_ge(xT_psum, 2 * u + 2)
                sp.dma_start(x_ring[k][:, :], unit_rows(x, u + RING)).then_inc(x_loaded[k], 16)

            def store_unit(u, k):
                sp.wait_ge(normed, u + 1)
                sp.dma_start(unit_rows(out, u), o_ring[k][:, :]).then_inc(stored[k], 16)

            def store_sums(c, g, slot, total):
                sp.wait_ge(sum_copied, total)
                sp.dma_start(c_dram[c][bass.ds(g * (G * P), G * P), :].rearrange("(k p) d -> p k d", p=P),
                             sums[slot][:, :, :]).then_inc(sums_stored[slot], 16)

            def body_a(i):
                for k in range(RING):
                    u = RING * i + k
                    load_unit(u, k)
                    if not isinstance(u, int) or u >= 2:
                        store_unit(u - 2, (k - 2) % RING)
                store_sums(0, i, 0, G * i + G)

            body_a(0)
            with sp.Fori(1, A_BODIES) as i:
                body_a(i)

            def body_b(i, last):
                for k in range(RING):
                    u = RING * i + k
                    if not last:
                        load_unit(u, k)
                    elif k == 0:
                        sp.wait_ge(xT_psum, 2 * u + 2)
                        sp.dma_start(x_ring[0][0:TAIL_P, 0:TAIL_RPP * D], tail_rows[0]).then_inc(x_loaded[0], 16)
                    store_unit(u - 2, (k - 2) % RING)
                    g = RING * (i - A_BODIES) + k
                    store_sums(1, g, k, TILES + G * g + G)

            with sp.Fori(A_BODIES, BODIES - 1) as i:
                body_b(i, False)
            body_b(BODIES - 1, True)
            for u in (UNITS - 2, UNITS - 1):
                store_unit(u, u % RING)
            sp.wait_ge(normed, UNITS + 1)
            sp.dma_start(tail_rows[1], o_ring[0][0:TAIL_P, 0:TAIL_RPP * D]).then_inc(stored[0], 16)
            for g in range(RING * B_BODIES, GROUPS):
                store_sums(1, g, g % RING, TILES + G * g + G)
            for k in range(RING):
                sp.wait_ge(sums_stored[k], 16 * ALL_STORES[k])

            def body_c(j):
                for k in range(2 * G):
                    n = 2 * G * j + k
                    until(sp, ta_psum, n - G + 1)
                    sp.dma_start(c1_in[k % G], c_dram[0][bass.ds(n * P, P), :]).then_inc(c1_loaded[k % G], 16)
                    until(sp, tb_psum, n - G + 1)
                    sp.dma_start(c2_in[k % G], c_dram[1][bass.ds(n * P, P), :]).then_inc(c2_loaded[k % G], 16)

            body_c(0)
            with sp.Fori(1, TILES // (2 * G)) as j:
                body_c(j)
            for k in range(RING):
                sp.wait_ge(stored[k], 16 * (BODIES + (k == 0)))
            for k in range(G):
                sp.wait_ge(scattered[k], 16 * GROUPS)

        @block.gpsimd
        def _(pool):
            pool.memset(ident[:, :], 0.0).then_inc(consts, 1)
            pool.wait_ge(consts, 1)
            pool.affine_select(out=ident[:, :], in_=ident[:, :], compare_op=ALU.not_equal, fill=1.0,
                               base=0, pattern=[[-1, P]], channel_multiplier=1).then_inc(identity_ready, 1)
            pool.iota(row_number[:, :], [[P, SLOTS]], base=0, channel_multiplier=1).then_inc(numbers_ready, 1)
            nought = pool.alloc_register("nought")
            bound = pool.alloc_register("bound")
            pool.reg_mov(nought, 0)

            def limit(rows):
                pool.reg_add(bound, nought, rows - 1)

            def gather(dest, table, rows, index, s):
                pool.indirect_dma_start(dest, None, table, bass.IndirectOffsetOnAxis(ap=index, axis=0),
                                        bounds_check=bound, oob_is_err=False).then_inc(s, 16)

            def scatter(table, source, index, s):
                pool.indirect_dma_start(table, bass.IndirectOffsetOnAxis(ap=index, axis=0), source, None,
                                        bounds_check=bound, oob_is_err=False).then_inc(s, 16)

            def gather_group(g, slot, table, rows):
                pool.wait_ge(gather_staged, g + 1)
                limit(rows)
                for k in range(G):
                    if not isinstance(g, int) or g > 0:
                        pool.wait_ge(summed, G * g - G + k + 1)
                        limit(rows)
                    gather(rows_in[k][:, :], table, rows, gather_idx[slot][:, k:k + 1], gathered[k])

            def body_a(i, look_up):
                gather_group(i, 0, x[:, :], N)
                pool.wait_ge(table_staged, i + 1)
                limit(N)
                for k in range(TABLE_OPS):
                    if look_up:
                        gather(found[:, k:k + 1], tail_of_node[0:N, :], N, table_idx[:, k:k + 1], table_done)
                    else:
                        scatter(tail_of_node[0:N, :], table_val[:, k:k + 1], table_idx[:, k:k + 1], table_done)

            pool.wait_ge(table_blank, 16)
            pool.wait_ge(blank, 6)
            body_a(0, False)
            with pool.Fori(1, HALF) as i:
                body_a(i, False)
            pool.wait_ge(table_done, 16 * TABLE_OPS * HALF)
            limit(N)
            with pool.Fori(HALF, GROUPS) as i:
                body_a(i, True)
            pool.wait_ge(sums_stored[0], 16 * A_STORES[0])
            limit(CROWS)
            with pool.Fori(0, B_BODIES) as m:
                for k in range(RING):
                    gather_group(GROUPS + RING * m + k, k, c_dram[0][:, :], CROWS)
            for g in range(RING * B_BODIES, GROUPS):
                gather_group(GROUPS + g, g % RING, c_dram[0][:, :], CROWS)

            for k in range(RING):
                pool.wait_ge(sums_stored[k], 16 * ALL_STORES[k])
            pool.wait_ge(normed, UNITS + 1)
            for k in range(RING):
                pool.wait_ge(stored[k], 16 * (BODIES + (k == 0)))
            limit(CROWS)

            LAG = 6

            def body_c(j):
                for k in range(2 * G):
                    n = 2 * G * j + k
                    if k % G == 0:
                        pool.wait_ge(gather_staged, 2 * GROUPS + 2 * j + k // G + 1)
                        limit(CROWS)
                    pool.wait_ge(summed, 2 * TILES + n - G + 1)
                    limit(CROWS)
                    gather(rows_in[k % G][:, :], c_dram[1][:, :], CROWS, gather_idx[k // G][:, k % G:k % G + 1],
                           gathered[k % G])
                    until(pool, ta_psum, n - G + 1)
                    limit(N)
                    gather(tail_x[k % G], x[:, :], N, tailx_idx[k // G][:, k % G:k % G + 1], tailx_in[k % G])
                    if not isinstance(j, int) or k >= LAG:
                        late = (k - LAG) % (2 * G)
                        pool.wait_ge(cnormed, n - LAG + 1)
                        limit(N)
                        pool.wait_ge(tailo_staged, 2 * j + (k - LAG) // G + 1)
                        limit(N)
                        scatter(out[:, :], co[late % G], tailo_idx[late // G][:, late % G:late % G + 1],
                                scattered[late % G])

            body_c(0)
            with pool.Fori(1, TILES // (2 * G)) as j:
                body_c(j)
            for n in range(TILES - LAG, TILES):
                late = n % (2 * G)
                pool.wait_ge(cnormed, n + 1)
                pool.wait_ge(tailo_staged, n // G + 1)
                scatter(out[:, :], co[late % G], tailo_idx[late // G][:, late % G:late % G + 1],
                                scattered[late % G])

        @block.scalar
        def _(act):
            def copy_xT(p, k, rows=P):
                act.wait_ge(xT_psum, p + 1)
                until(act, y_psum, p - 1)
                view = [t[:, :].rearrange("p (q c) -> p q c", c=P)[:, :, 0:rows] for t in (xT[k % 2], ps_xT[k % 2])]
                act.copy(view[0], view[1]).then_inc(xT_copied, 1)

            def roots(u, slot, rows=P, tiles=RPP):
                act.wait_ge(var_ready, u + 1)
                act.activation(std[slot][0:rows, 0:tiles], mean_var[slot][0:rows, 0:tiles, 1], ACT.Sqrt,
                               bias=eps[0:rows, :]).then_inc(std_ready, 1)

            def normalise(u, slot, turn, rows=P, tiles=RPP):
                act.wait_ge(shift_ready, u + 1)
                until(act, stored[slot], 16 * turn)
                for r in range(tiles):
                    last = act.activation(o_ring[slot][0:rows, r * D:(r + 1) * D], y_ring[slot][0:rows, r * D:(r + 1) * D],
                                          ACT.Identity, bias=shift[slot][0:rows, r:r + 1],
                                          scale=rstd[slot][0:rows, r:r + 1])
                last.then_inc(normed, 1)

            def unit(u, i, k):
                copy_xT(2 * u, 0)
                copy_xT(2 * u + 1, 1)
                if not isinstance(u, int) or u >= 1:
                    roots(u - 1, (k - 1) % RING)
                if not isinstance(u, int) or u >= 2:
                    normalise(u - 2, (k - 2) % RING, i - (k < 2))

            act.wait_ge(blank, 6)
            for u in range(2 * RING):
                unit(u, u // RING, u % RING)
            with act.Fori(2, BODIES) as i:
                for k in range(RING):
                    unit(RING * i + k, i, k)
            copy_xT(2 * UNITS, 0, TAIL_P)
            roots(UNITS - 1, 2)
            normalise(UNITS - 2, 1, BODIES - 1)
            roots(UNITS, 0, TAIL_P, TAIL_RPP)
            normalise(UNITS - 1, 2, BODIES - 1)
            normalise(UNITS, 0, BODIES, TAIL_P, TAIL_RPP)

            act.wait_ge(normed, UNITS + 1)
            for k in range(RING):
                act.wait_ge(stored[k], 16 * (BODIES + (k == 0)))

            def c_roots(n, k):
                act.wait_ge(cvar_ready, n + 1)
                act.activation(cstd[k % G][:, :], cmv[k % G][:, 1:2], ACT.Sqrt, bias=eps[:, :]).then_inc(cstd_ready, 1)

            def c_normalise(n, k, turn):
                act.wait_ge(cshift_ready, n + 1)
                until(act, scattered[k % G], 16 * turn)
                act.activation(co[k % G], cy[k % G], ACT.Identity, bias=cshift[k % G][:, :],
                               scale=crstd[k % G][:, :]).then_inc(cnormed, 1)

            def c_tile(n, j, k):
                act.wait_ge(ta_psum, n + 1)
                until(act, cy_psum, n - 1)
                act.copy(catT[k % 2][:, 0:2 * D], ps_xT[0][:, :]).then_inc(ta_copied, 1)
                if not isinstance(n, int) or n >= 2:
                    c_roots(n - 2, (k - 2) % G)
                act.wait_ge(tb_psum, n + 1)
                act.copy(catT[k % 2][:, 2 * D:4 * D], ps_xT[1][:, :]).then_inc(tb_copied, 1)
                if not isinstance(n, int) or n >= 3:
                    c_normalise(n - 3, (k - 3) % G, j - (k < 3))

            for n in range(2 * G):
                c_tile(n, n // G, n % G)
            with act.Fori(2, TILES // G) as j:
                for k in range(G):
                    c_tile(G * j + k, j, k)
            c_roots(TILES - 2, (TILES - 2) % G)
            c_normalise(TILES - 3, (TILES - 3) % G, GROUPS - 1)
            c_roots(TILES - 1, (TILES - 1) % G)
            c_normalise(TILES - 2, (TILES - 2) % G, GROUPS - 1)
            c_normalise(TILES - 1, (TILES - 1) % G, GROUPS - 1)

        @block.tensor
        def _(pe):
            pe.wait_ge(identity_ready, 1)
            pe.wait_ge(floats_ready, 4)
            for bank, lists in zip((ps_xT[0], ps_xT[1], ps_y[0], ps_y[1]), (dst_f, next_f, src_f, w_l)):
                for h in range(2):
                    last = pe.transpose(bank[:, h * P:(h + 1) * P], lists[:, h, :], ident[:, :])
            last.then_inc(lists_turned, 1)
            pe.wait_ge(tables_ready, 1)
            pe.wait_ge(w0_ready, KC)

            def turn_pair(p, k, i, rows=P):
                slot, half = k // 2, k % 2
                if half == 0:
                    pe.wait_ge(x_loaded[slot], 16 * i + 16)
                until(pe, xT_copied, p - 1)
                for r in range(2):
                    for c in range(KC):
                        at = (2 * half + r) * D + c * P
                        q = r * KC + c
                        last = pe.transpose(ps_xT[half][:, q * P:q * P + rows], x_ring[slot][0:rows, at:at + P],
                                            ident[0:rows, 0:rows])
                return last.then_inc(xT_psum, 1)

            def multiply_pair(p, half, rows=P):
                pe.wait_ge(xT_copied, p + 1)
                until(pe, y_copied, p - 1)
                for r in range(2):
                    for c in range(KC):
                        q = r * KC + c
                        last = pe.matmul(ps_y[half][0:rows, r * D:(r + 1) * D], xT[half][:, q * P:q * P + rows],
                                         w_sb[:, c, :], start=c == 0, stop=c == KC - 1)
                last.then_inc(y_psum, 1)

            def sum_tile(e, k):
                pe.wait_ge(sel_ready, e + 1)
                pe.wait_ge(carry_ready, e + 1)
                until(pe, sum_copied, e - 1)
                pe.matmul(ps_sum[k % 2][:, 0:D], sel[k % G][:, :], rows_in[k % G][:, :],
                          start=True, stop=True).then_inc(summed, 1)

            def body(i, tiles_after):
                for k in range(2 * RING):
                    p = 2 * RING * i + k
                    turn_pair(p, k, i)
                    if not isinstance(p, int) or p >= 1:
                        multiply_pair(p - 1, (k - 1) % 2)
                    for e, ke in tiles_after[k]:
                        sum_tile(e, ke)

            def body_a(i):
                body(i, [[], []] + [[(G * i + k, k)] for k in range(G)])

            def body_b(i):
                e = TILES + RING * G * (i - A_BODIES)
                body(i, [[(e + 2 * k + r, 2 * (k % 2) + r) for r in range(2)] for k in range(2 * RING)])

            body_a(0)
            with pe.Fori(1, A_BODIES) as i:
                body_a(i)
            with pe.Fori(A_BODIES, BODIES) as i:
                body_b(i)
            turn_pair(2 * UNITS, 0, BODIES, TAIL_P)
            multiply_pair(2 * UNITS - 1, 1)
            multiply_pair(2 * UNITS, 0, TAIL_P)
            with pe.Fori(RING * B_BODIES, GROUPS) as g:
                for k in range(G):
                    sum_tile(TILES + G * g + k, k)

            pe.wait_ge(xT_copied, PAIRS)
            pe.wait_ge(y_copied, PAIRS)

            def turn_c(n, k):
                until(pe, ta_copied, n)
                for r, rows in enumerate((tail_x[k % G], c1_in[k % G])):
                    for c in range(KC):
                        q = r * KC + c
                        last = pe.transpose(ps_xT[0][:, q * P:(q + 1) * P], rows[:, c * P:(c + 1) * P], ident[:, :])
                last.then_inc(ta_psum, 1)

            def turn_d(n, k):
                until(pe, tb_copied, n)
                for r, rows in enumerate((c2_in[k % G], sums[0][:, k % G, :])):
                    for c in range(KC):
                        q = r * KC + c
                        last = pe.transpose(ps_xT[1][:, q * P:(q + 1) * P], rows[:, c * P:(c + 1) * P], ident[:, :])
                last.then_inc(tb_psum, 1)

            def multiply_c(n, k, part):
                if part == 0:
                    pe.wait_ge(ta_copied, n + 1)
                    until(pe, cy_copied, n - 1)
                else:
                    pe.wait_ge(tb_copied, n + 1)
                half = BLOCKS * KC // 2
                for q in range(part * half, part * half + half):
                    last = pe.matmul(ps_y[k % 2][:, 0:D], catT[k % 2][:, q * P:(q + 1) * P], w_sb[:, q, :],
                                     start=q == 0, stop=q == 2 * half - 1)
                if part == 1:
                    last.then_inc(cy_psum, 1)

            def c_tile(j, n, k):
                sum_tile(2 * TILES + n, k)
                pe.wait_ge(tailx_in[k % G], 16 * j + 16)
                pe.wait_ge(c1_loaded[k % G], 16 * j + 16)
                turn_c(n, k)
                if not isinstance(n, int) or n >= 1:
                    multiply_c(n - 1, k - 1, 0)
                pe.wait_ge(c2_loaded[k % G], 16 * j + 16)
                pe.wait_ge(sum_copied, 2 * TILES + n + 1)
                turn_d(n, k)
                if not isinstance(n, int) or n >= 1:
                    multiply_c(n - 1, k - 1, 1)

            for k in range(G):
                c_tile(0, k, k)
            with pe.Fori(1, TILES // G) as j:
                for k in range(G):
                    c_tile(j, G * j + k, k)
            multiply_c(TILES - 1, TILES - 1, 0)
            multiply_c(TILES - 1, TILES - 1, 1)

        @block.vector
        def _(dve):
            dve.memset(dst_i[:, :, :], -1).then_inc(blank, 1)
            dve.memset(next_i[:, :, :], -1).then_inc(blank, 1)
            dve.memset(src_i[:, :, :], ABSENT).then_inc(blank, 1)
            dve.memset(absent[:, :], ABSENT).then_inc(blank, 1)
            dve.memset(w_l[:, :, 1:P], 0.0)
            dve.memset(w_l[:, :, 0:1], 1.0).then_inc(blank, 1)
            dve.memset(found[:, :], ABSENT)
            dve.memset(src_tail[:, :], ABSENT)
            for k in range(G):
                dve.memset(rows_in[k][:, :], 0.0)
            dve.memset(eps[:, :], EPS).then_inc(blank, 1)
            dve.wait_ge(edges_loaded, 16 * 17)
            dve.tensor_copy(dst_f[:, :, :], dst_i[:, :, :]).then_inc(floats_ready, 1)
            dve.tensor_copy(next_f[:, :, :], next_i[:, :, :]).then_inc(floats_ready, 1)
            dve.tensor_copy(src_f[:, :, :], src_i[:, :, :]).then_inc(floats_ready, 1)
            dve.tensor_copy(keys_f[:, :, 1:P], dst_i[:, :, 1:P])
            dve.tensor_copy(keys_f[:, :, 0:1], dst_i[:, :, P - 1:P]).then_inc(floats_ready, 1)
            dve.wait_ge(weights_loaded, 48)
            dve.wait_ge(identity_ready, 1)
            for c in range(KC):
                dve.tensor_tensor(w_sb[:, c, c * P:(c + 1) * P], w_sb[:, c, c * P:(c + 1) * P], ident[:, :],
                                  ALU.add).then_inc(w0_ready, 1)
            dve.wait_ge(lists_turned, 1)
            dve.tensor_copy(key_in[:, :], ps_xT[0][:, 0:SLOTS]).then_inc(table_chain, 1)
            dve.tensor_copy(src_node[:, :], ps_y[0][:, 0:SLOTS])
            dve.tensor_copy(w1[:, :], ps_y[1][:, 0:SLOTS])
            dve.wait_ge(table_chain, 1)
            dve.tensor_tensor(tail_f[:, :], key_in[:, :], ps_xT[1][:, 0:SLOTS], ALU.is_equal).then_inc(table_chain, 1)
            dve.wait_ge(table_chain, 2)
            dve.scalar_tensor_tensor(out=tail_node[:, :], in0=tail_f[:, :], scalar=float(ABSENT), in1=key_in[:, :],
                                     op0=ALU.mult, op1=ALU.add).then_inc(table_chain, 1)
            dve.wait_ge(table_chain, 3)
            dve.memset(tail_node[0:1, :], ABSENT).then_inc(tables_ready, 1)
            dve.wait_ge(tables_ready, 1)
            dve.wait_ge(numbers_ready, 1)

            def columns(dest, table, t, n):
                return dve.tensor_scalar(dest, table[:, bass.ds(t, n)], 0, None, ALU.add)

            def copy_y(p, u, slot, half, rows=P):
                dve.wait_ge(y_psum, p + 1)
                until(dve, normed, u - RING + 1)
                dve.tensor_tensor(y_ring[slot][0:rows, half * 2 * D:(half + 1) * 2 * D], ps_y[half][0:rows, :],
                                  bias2[0:rows, :], ALU.add).then_inc(y_copied, 1)

            def unit_stats(p, slot, half, rows=P):
                dve.wait_ge(y_copied, p + 1)
                for r in (2 * half, 2 * half + 1):
                    last = dve.bn_stats(stats[slot][0:rows, r, :], y_ring[slot][0:rows, r * D:(r + 1) * D])
                last.then_inc(stats_ready, 1)

            def unit_inverse(u, slot, rows=P, tiles=RPP):
                dve.wait_ge(std_ready, u + 1)
                dve.reciprocal(rstd[slot][0:rows, 0:tiles], std[slot][0:rows, 0:tiles]).then_inc(rstd_ready, 1)

            def unit_variance(slot, rows=P, tiles=RPP):
                for r in range(tiles):
                    last = dve.bn_aggr(mean_var[slot][0:rows, r, :], stats[slot][0:rows, r, :])
                last.then_inc(var_ready, 1)

            def unit_shift(u, slot, rows=P, tiles=RPP):
                dve.wait_ge(rstd_ready, u + 1)
                dve.scalar_tensor_tensor(out=shift[slot][0:rows, 0:tiles], in0=mean_var[slot][0:rows, 0:tiles, 0],
                                         scalar=-1.0, in1=rstd[slot][0:rows, 0:tiles], op0=ALU.mult,
                                         op1=ALU.mult).then_inc(shift_ready, 1)

            def unit_end(u, k):
                dve.wait_ge(stats_ready, 2 * u + 2)
                if not isinstance(u, int) or u >= 1:
                    unit_inverse(u - 1, (k - 1) % RING)
                unit_variance(k)
                if not isinstance(u, int) or u >= 1:
                    unit_shift(u - 1, (k - 1) % RING)

            def select(e, k, t, weights):
                until(dve, summed, e - G + 1)
                dve.tensor_scalar(sel[k % G][:, :], keys_out[:, bass.ds(t * P, P)], key_in[:, bass.ds(t, 1)],
                                  weights[:, bass.ds(t, 1)], ALU.is_equal, ALU.mult).then_inc(sel_ready, 1)

            def carry(e, g, k, before):
                dve.wait_ge(gathered[k], 16 * g + 16)
                if before is None:
                    dve.memset(rows_in[k][0:1, :], 0.0).then_inc(carry_ready, 1)
                else:
                    dve.wait_ge(sum_copied, e)
                    dve.tensor_copy(rows_in[k][0:1, :], before[0:1, (k - 1) % G, :]).then_inc(carry_ready, 1)

            def copy_sum(e, k, slot, uses):
                dve.wait_ge(summed, e + 1)
                if k == 0:
                    until(dve, sums_stored[slot], 16 * uses)
                dve.tensor_copy(sums[slot][:, k, :], ps_sum[k % 2][:, 0:D]).then_inc(sum_copied, 1)

            def stage_table(i, look_up):
                until(dve, table_done, 16 * TABLE_OPS * i)
                if look_up:
                    if not isinstance(i, int) or i > HALF:
                        columns_found(i - HALF - 1)
                    columns(table_idx[:, :], src_node, TABLE_OPS * (i - HALF), TABLE_OPS).then_inc(table_staged, 1)
                else:
                    columns(table_idx[:, :], tail_node, TABLE_OPS * i, TABLE_OPS)
                    columns(table_val[:, :], row_number, TABLE_OPS * i, TABLE_OPS).then_inc(table_staged, 1)

            def columns_found(q):
                dve.tensor_scalar(src_tail[:, bass.ds(TABLE_OPS * q, TABLE_OPS)], found[:, :], 0, None,
                                  ALU.add).then_inc(found_copied, 1)

            def copy_and_measure(i, k):
                u, slot, half = RING * i + k // 2, k // 2, k % 2
                copy_y(2 * RING * i + k, u, slot, half)
                unit_stats(2 * RING * i + k, slot, half)
                if half:
                    unit_end(u, slot)

            def body_a(i, look_up):
                e = G * i
                columns(gather_idx[0][:, :], src_node, G * i, G).then_inc(gather_staged, 1)
                copy_and_measure(i, 0)
                stage_table(i, look_up)
                for k in range(G):
                    select(e + k, k, G * i + k, w1)
                for k in range(G):
                    carry(e + k, i, k, None if isinstance(e, int) and e + k == 0 else sums[0])
                    copy_and_measure(i, k + 1)
                    copy_sum(e + k, k, 0, i)
                copy_and_measure(i, G + 1)

            dve.wait_ge(keys_loaded, 16)
            body_a(0, False)
            with dve.Fori(1, HALF) as i:
                body_a(i, False)
            body_a(HALF, True)
            with dve.Fori(HALF + 1, GROUPS) as i:
                body_a(i, True)
            dve.wait_ge(table_done, 16 * TABLE_OPS * GROUPS)
            columns_found(HALF - 1)
            dve.wait_ge(found_copied, HALF)
            dve.scalar_tensor_tensor(out=w2[:, 0:TILES], in0=src_tail[:, 0:TILES], scalar=float(CROWS),
                                     in1=w1[:, 0:TILES], op0=ALU.is_lt, op1=ALU.mult).then_inc(w2_ready, 1)
            dve.wait_ge(w2_ready, 1)
            dve.memset(w2[0:1, 0:TILES], 1.0).then_inc(w2_ready, 1)
            dve.wait_ge(w2_ready, 2)
            columns(gather_idx[0][:, :], src_tail, 0, G).then_inc(gather_staged, 1)

            def group_b(g, slot, uses, first, last, dense):
                e = TILES + G * g
                if not last:
                    columns(gather_idx[(slot + 1) % RING][:, :], src_tail, G * g + G, G).then_inc(gather_staged, 1)
                for k in range(G):
                    select(e + k, k, G * g + k, w2)
                for k in range(G):
                    before = sums[slot if k else (slot - 1) % RING]
                    carry(e + k, GROUPS + g, k, None if first and k == 0 else before)
                    copy_sum(e + k, k, slot, uses)
                    if k % 2 and dense is not None:
                        copy_and_measure(dense, 2 * slot + k // 2)

            def body_b(i, first):
                for slot in range(RING):
                    group_b(RING * (i - A_BODIES) + slot, slot, A_STORES[slot] + i - A_BODIES,
                            first and slot == 0, False, i)

            body_b(A_BODIES, True)
            with dve.Fori(A_BODIES + 1, BODIES) as i:
                body_b(i, False)
            copy_y(2 * UNITS, UNITS, 0, 0, TAIL_P)
            unit_stats(2 * UNITS, 0, 0, TAIL_P)
            dve.wait_ge(stats_ready, 2 * UNITS + 1)
            unit_inverse(UNITS - 1, RING - 1)
            unit_variance(0, TAIL_P, TAIL_RPP)
            unit_shift(UNITS - 1, RING - 1)
            unit_inverse(UNITS, 0, TAIL_P, TAIL_RPP)
            unit_shift(UNITS, 0, TAIL_P, TAIL_RPP)
            for g in range(RING * B_BODIES, GROUPS):
                group_b(g, g % RING, A_STORES[g % RING] + g // RING, False, g == GROUPS - 1, None)

            dve.wait_ge(normed, UNITS + 1)
            for k in range(RING):
                dve.wait_ge(sums_stored[k], 16 * ALL_STORES[k])

            def stage_c(g, half):
                columns(tailx_idx[half][:, :], tail_node, G * g, G)
                columns(gather_idx[half][:, :], src_tail, G * g, G).then_inc(gather_staged, 1)

            def c_sum(n, k, half):
                e = 2 * TILES + n
                select(e, k, n, w2)
                carry(e, 2 * GROUPS + half, k, None if isinstance(n, int) and n == 0 else sums[0])
                dve.wait_ge(summed, e + 1)
                until(dve, tb_psum, n - G + 1)
                dve.tensor_copy(sums[0][:, k, :], ps_sum[k % 2][:, 0:D]).then_inc(sum_copied, 1)

            def c_copy(n, k):
                dve.wait_ge(cy_psum, n + 1)
                until(dve, cnormed, n - G + 1)
                dve.tensor_tensor(cy[k % G], ps_y[k % 2][:, 0:D], bias2[:, 0:D], ALU.add).then_inc(cy_copied, 1)
                dve.wait_ge(cy_copied, n + 1)
                dve.bn_stats(cstats[k % G][:, :], cy[k % G]).then_inc(cstats_ready, 1)

            def c_inverse(n, k):
                dve.wait_ge(cstd_ready, n + 1)
                dve.reciprocal(crstd[k % G][:, :], cstd[k % G][:, :]).then_inc(crstd_ready, 1)

            def c_variance(k):
                dve.bn_aggr(cmv[k % G][:, :], cstats[k % G][:, :]).then_inc(cvar_ready, 1)

            def c_shift(n, k):
                dve.wait_ge(crstd_ready, n + 1)
                dve.scalar_tensor_tensor(out=cshift[k % G][:, :], in0=cmv[k % G][:, 0:1], scalar=-1.0,
                                         in1=crstd[k % G][:, :], op0=ALU.mult, op1=ALU.mult).then_inc(cshift_ready, 1)

            def c_finish(n, k):
                if not isinstance(n, int) or n >= 1:
                    c_copy(n - 1, k - 1)
                    dve.wait_ge(cstats_ready, n)
                    if not isinstance(n, int) or n >= 2:
                        c_inverse(n - 2, k - 2)
                    c_variance(k - 1)
                    if not isinstance(n, int) or n >= 2:
                        c_shift(n - 2, k - 2)

            def body_c(j):
                for k in range(2 * G):
                    n, g = 2 * G * j + k, 2 * j + k // G
                    if k % G == 0:
                        for q in range(G):
                            until(dve, tailx_in[q], 16 * g)
                        stage_c(g + 1, (k // G + 1) % 2)
                    if k % G == 1:
                        for q in range(G):
                            until(dve, scattered[q], 16 * (g - 1))
                        columns(tailo_idx[k // G][:, :], tail_node, G * g, G).then_inc(tailo_staged, 1)
                    c_sum(n, k % G, g)
                    c_finish(n, k)

            stage_c(0, 0)
            body_c(0)
            with dve.Fori(1, TILES // (2 * G)) as j:
                body_c(j)
            c_finish(TILES, TILES)
            c_inverse(TILES - 1, TILES - 1)
            c_shift(TILES - 1, TILES - 1)


_INS = ["x", "src", "dst", "edge_weight", "L0_gnn_shared_weight", "L0_gnn_output_bias"]


def kernel(**inputs):
    import numpy as _np
    import concourse.bacc as _bacc
    from concourse import mybir as _mybir
    from concourse.bass_utils import run_bass_kernel_spmd as _run

    nc = _bacc.Bacc("TRN2", target_bir_lowering=False, num_devices=1)
    arrays, args = {}, []
    for name in _INS:
        a = _np.ascontiguousarray(inputs[name])
        arrays[f"in_{name}"] = a
        args.append(nc.dram_tensor(f"in_{name}", a.shape, _mybir.dt.from_np(a.dtype), kind="ExternalInput").ap())
    out = nc.dram_tensor("out_rows", inputs["x"].shape, _mybir.dt.float32, kind="ExternalOutput").ap()
    gnn_program(nc, *args, out)
    r = _run(nc, [arrays], core_ids=[0])
    return r.results[0]["out_rows"]
```

```python
def gnn_program(nc, x, src, dst, edge_weight, weight, bias, out):
    import concourse.bass as bass
    from concourse import mybir
    from contextlib import ExitStack

    f32, i32 = mybir.dt.float32, mybir.dt.int32
    ALU = mybir.AluOpType
    ACT = mybir.ActivationFunctionType

    N, D = x.shape
    E = src.shape[0]
    P = 128
    KC = D // P
    BLOCKS = weight.shape[0] // D
    EPS = 1e-5

    RPP = 4
    UROWS = P * RPP
    UNITS = N // UROWS
    TAIL_ROWS = N - UNITS * UROWS
    TAIL_RPP = 2
    TAIL_P = TAIL_ROWS // TAIL_RPP
    assert TAIL_P * TAIL_RPP == TAIL_ROWS and TAIL_P % 16 == 0
    RING = 3
    BODIES = UNITS // RING
    assert BODIES * RING == UNITS

    EPT = P - 1
    G = 4
    TILES = -(-E // EPT)
    TILES += -TILES % (2 * G)
    GROUPS = TILES // G
    FULL = E // EPT
    REST = E - FULL * EPT
    SLOTS = 2 * P
    assert 0 < REST < EPT and P < FULL < SLOTS - 1 and TILES <= SLOTS
    GB = 4
    B_BODIES = GROUPS // GB
    A_START = BODIES - GROUPS - B_BODIES
    B_START = A_START + GROUPS
    B_REST = GROUPS - B_BODIES * GB
    assert A_START == 3 and 0 < B_REST < GB
    TABLE_OPS = 10
    STEPS = TILES // TABLE_OPS
    LISTED = A_START + 2 * STEPS
    LIST_END = A_START + 3 * STEPS
    assert STEPS * TABLE_OPS == TILES and LISTED < B_START < LIST_END < BODIES
    ABSENT = 1 << 23
    CROWS = TILES * P
    TABLE_COLS = -(-N // P)
    CB = 2 * G
    C_BODIES_MAX = TILES // CB
    FIELDS = 4

    v_dram = nc.dram_tensor("v_rows", (CROWS, D), f32).ap()
    list_dram = nc.dram_tensor("packed_edges", (TILES * P, FIELDS), f32).ap()
    keys_out2_dram = nc.dram_tensor("keys_out2", (SLOTS * P,), f32).ap()
    c_dram = [nc.dram_tensor(f"c{n}_rows", (CROWS, D), f32).ap() for n in (1, 2)]
    tail_of_node = nc.dram_tensor("tail_of_node", (TABLE_COLS * P, 1), i32).ap()
    keys_out_dram = nc.dram_tensor("keys_out", (SLOTS * P,), f32).ap()

    ctx = ExitStack()
    with ctx:
        def sb(name, shape, dt=f32):
            return ctx.enter_context(nc.sbuf_tensor(name, shape, dt))

        def pb(name):
            return ctx.enter_context(nc.psum_tensor(name, [P, 2 * D], f32))

        def sem(name):
            return ctx.enter_context(nc.semaphore(name))

        def sems(name, n):
            return [sem(f"{name}{k}") for k in range(n)]

        ident = sb("ident", [P, P])
        w_sb = sb("w_sb", [P, BLOCKS * KC, D])
        bias4 = sb("bias4", [P, RPP * D])
        bias2 = bias4[:, 0:2 * D]
        ones = sb("ones", [P, P])
        below = sb("below", [P, P])
        below_tile = sb("below_tile", [P, 2, SLOTS])
        eps = sb("eps", [P, 1])
        x_ring = [sb(f"x_ring{k}", [P, RPP * D]) for k in range(RING)]
        xT = [sb(f"xT{k}", [P, 2 * D]) for k in range(2)]
        y_ring = [sb(f"y_ring{k}", [P, RPP * D]) for k in range(RING)]
        o_ring = [sb(f"o_ring{k}", [P, RPP * D]) for k in range(RING)]
        stats = [sb(f"stats{k}", [P, RPP, 6]) for k in range(RING)]
        mean_var = [sb(f"mean_var{k}", [P, RPP, 2]) for k in range(RING)]
        std = [sb(f"std{k}", [P, RPP]) for k in range(RING)]
        rstd = [sb(f"rstd{k}", [P, RPP]) for k in range(RING)]
        shift = [sb(f"shift{k}", [P, RPP]) for k in range(RING)]
        rows_in = [sb(f"rows_in{k}", [P, D]) for k in range(G)]
        sums = [sb(f"sums{k}", [P, G, D]) for k in range(GB)]
        sel = [sb(f"sel{k}", [P, P]) for k in range(G)]
        keys_out = sb("keys_out_bc", [P, TILES * P])
        dst_i = sb("dst_i", [P, 2, P], i32)
        next_i = sb("next_i", [P, 2, P], i32)
        src_i = sb("src_i", [P, 2, P], i32)
        w_l = sb("w_l", [P, 2, P])
        dst_f = sb("dst_f", [P, 2, P])
        next_f = sb("next_f", [P, 2, P])
        src_f = sb("src_f", [P, 2, P])
        keys_f = sb("keys_f", [P, 2, P])
        own_r = sb("own_r", [P, 2, P])
        row_r = sb("row_r", [P, 2, P])
        key_in = sb("key_in", [P, SLOTS])
        w1 = sb("w1", [P, SLOTS])
        w2 = sb("w2", [P, SLOTS])
        src_node = sb("src_node", [P, SLOTS], i32)
        tail_node = sb("tail_node", [P, SLOTS], i32)
        tail_f = sb("tail_f", [P, SLOTS])
        row_number = sb("row_number", [P, SLOTS], i32)
        src_tail = sb("src_tail", [P, SLOTS], i32)
        own_T = next_i[:, :, :].rearrange("p h c -> p (h c)").bitcast(f32)
        own = sb("own", [P, SLOTS])
        later = sb("later", [1, SLOTS])
        not_padding = sb("not_padding", [P, SLOTS])
        active = sb("active", [P, SLOTS])
        inactive = src_i[:, :, :].rearrange("p h c -> p (h c)").bitcast(f32)
        place_f = dst_i[:, :, :].rearrange("p h c -> p (h c)").bitcast(f32)
        place = sb("place", [P, SLOTS], i32)
        totals = sb("totals", [P, 2])
        totals_bc = sb("totals_bc", [P, 2, P])
        total = sb("total", [1, 1])
        body_starts = sb("body_starts", [1, C_BODIES_MAX])
        started = sb("started", [1, C_BODIES_MAX])
        bodies_f = sb("bodies_f", [1, 1])
        more_bodies = sb("more_bodies", [1, 1], i32)
        packed = x_ring[1][:, :].rearrange("p (h c f) -> p h c f", h=2, f=FIELDS)
        packed_next = sb("packed_next", [P, 2])
        key_in2 = sb("key_in2", [P, SLOTS])
        w_packed = sb("w_packed", [P, SLOTS])
        src_tail2 = sb("src_tail2", [P, SLOTS], i32)
        own2 = sb("own2", [P, SLOTS], i32)
        record = sb("record", [P, TABLE_OPS, FIELDS])
        gather_idx = [sb(f"gather_idx{k}", [P, G], i32) for k in range(GB)]
        tailx_idx = [sb(f"tailx_idx{k}", [P, G], i32) for k in range(2)]
        tailo_idx = [sb(f"tailo_idx{k}", [P, G], i32) for k in range(2)]
        table_idx = sb("table_idx", [P, TABLE_OPS], i32)
        table_val = sb("table_val", [P, TABLE_OPS], i32)
        found = sb("found", [P, TABLE_OPS], i32)
        list_blank = sums[2][:, :, :].rearrange("p g d -> p (g d)")[:, 0:TILES * FIELDS]
        absent = sums[3][:, :, :].rearrange("p g d -> p (g d)").bitcast(i32)[:, 0:TABLE_COLS]
        own_c2 = [o_ring[1][:, k * D:(k + 1) * D] for k in range(G)]
        v_out = [o_ring[2][:, k * D:(k + 1) * D] for k in range(G)]
        tail_x = [x_ring[0][:, k * D:(k + 1) * D] for k in range(G)]
        c1_in = [x_ring[1][:, k * D:(k + 1) * D] for k in range(G)]
        v_in = [x_ring[2][:, k * D:(k + 1) * D] for k in range(G)]
        cy = [y_ring[2][:, k * D:(k + 1) * D] for k in range(G)]
        co = [o_ring[0][:, k * D:(k + 1) * D] for k in range(G)]
        cstats = [sb(f"cstats{k}", [P, 6]) for k in range(G)]
        cmv = [sb(f"cmv{k}", [P, 2]) for k in range(G)]
        cstd = [sb(f"cstd{k}", [P, 1]) for k in range(G)]
        crstd = [sb(f"crstd{k}", [P, 1]) for k in range(G)]
        cshift = [sb(f"cshift{k}", [P, 1]) for k in range(G)]

        ps_xT = [pb(f"ps_xT{k}") for k in range(2)]
        ps_y = [pb(f"ps_y{k}") for k in range(2)]
        ps_sum = [pb(f"ps_sum{k}") for k in range(2)]
        ps_list = [pb(f"ps_list{k}") for k in range(2)]

        blank = sem("blank")
        consts = sem("consts")
        edges_loaded = sem("edges_loaded")
        weights_loaded = sem("weights_loaded")
        identity_ready = sem("identity_ready")
        w0_ready = sem("w0_ready")
        floats_ready = sem("floats_ready")
        keys_stored = sem("keys_stored")
        keys_loaded = sem("keys_loaded")
        lists_turned = sem("lists_turned")
        table_chain = sem("table_chain")
        tables_ready = sem("tables_ready")
        numbers_ready = sem("numbers_ready")
        table_blank = sem("table_blank")
        x_loaded = sems("x_loaded", RING)
        xT_psum = sem("xT_psum")
        xT_copied = sem("xT_copied")
        y_psum = sem("y_psum")
        y_copied = sem("y_copied")
        stats_ready = sem("stats_ready")
        var_ready = sem("var_ready")
        std_ready = sem("std_ready")
        rstd_ready = sem("rstd_ready")
        shift_ready = sem("shift_ready")
        normed = sem("normed")
        stored = sems("stored", RING)
        gather_staged = sem("gather_staged")
        gathered = sems("gathered", G)
        sel_ready = sem("sel_ready")
        carry_ready = sem("carry_ready")
        summed = sem("summed")
        sum_copied = sem("sum_copied")
        sums_stored = sems("sums_stored", GB)
        table_staged = sem("table_staged")
        table_done = sem("table_done")
        found_copied = sem("found_copied")
        w2_ready = sem("w2_ready")
        v_blank = sem("v_blank")
        own_chain = sem("own_chain")
        own_turned = sem("own_turned")
        later_ready = sem("later_ready")
        later_spread = sem("later_spread")
        active_ready = sem("active_ready")
        counted = sem("counted")
        totals_ready = sem("totals_ready")
        based = sem("based")
        place_chain = sem("place_chain")
        bodies_ready = sem("bodies_ready")
        packed_blank = sem("packed_blank")
        packed_loaded = sem("packed_loaded")
        packed_floats = sem("packed_floats")
        packed_turned = sem("packed_turned")
        packed_tables = sem("packed_tables")
        keys2_stored = sem("keys2_stored")
        keys2_loaded = sem("keys2_loaded")
        v_staged = sem("v_staged")
        own_gathered = sems("own_gathered", G)
        t_psum = sem("t_psum")
        t_copied = sem("t_copied")
        v_psum = sem("v_psum")
        v_copied = sem("v_copied")
        v_scattered = sems("v_scattered", G)
        tailx_staged = sem("tailx_staged")
        tailo_staged = sem("tailo_staged")
        tailx_in = sems("tailx_in", G)
        c1_loaded = sems("c1_loaded", G)
        v_loaded = sems("v_loaded", G)
        ta_psum = sem("ta_psum")
        ta_copied = sem("ta_copied")
        cy_psum = sem("cy_psum")
        cy_copied = sem("cy_copied")
        cstats_ready = sem("cstats_ready")
        cvar_ready = sem("cvar_ready")
        cstd_ready = sem("cstd_ready")
        crstd_ready = sem("crstd_ready")
        cshift_ready = sem("cshift_ready")
        cnormed = sem("cnormed")
        scattered = sems("scattered", G)

        ctx.enter_context(nc.allow_non_contiguous_dma(reason="a few hundred single keys and four-byte table entries"))
        block = ctx.enter_context(nc.Block())

        A_STORES = [GROUPS * (k == 0) for k in range(GB)]
        ALL_STORES = [A_STORES[k] + B_BODIES + (k < B_REST) for k in range(GB)]
        B_TILES = [range(GB * G * k // (2 * RING), GB * G * (k + 1) // (2 * RING)) for k in range(2 * RING)]
        AB_TILES, AB_GROUPS = 2 * TILES, 2 * GROUPS

        def until(eng, s, value):
            if not isinstance(value, int) or value > 0:
                eng.wait_ge(s, value)

        def body_count(eng):
            eng.wait_ge(bodies_ready, 1)
            return eng.value_load(more_bodies[0:1, 0:1], min_val=0, max_val=C_BODIES_MAX - 2) + 2

        PAIRS = 2 * UNITS + 1

        def unit_rows(ap, u):
            return ap[bass.ds(u * UROWS, UROWS), :].rearrange("(p r) d -> p (r d)", r=RPP)

        tail_rows = [ap[UNITS * UROWS:N, :].rearrange("(p r) d -> p (r d)", r=TAIL_RPP) for ap in (x, out)]

        @block.sync
        def _(sp):
            def as_column(ap):
                return ap.rearrange("(t o) -> t o", o=1)

            sp.dma_start(x_ring[0][:, :], unit_rows(x, 0)).then_inc(x_loaded[0], 16)
            sp.dma_start(w_sb[:, :, :], weight.rearrange("(c p) n -> p c n", p=P)).then_inc(weights_loaded, 16)
            for k in range(RPP):
                sp.dma_start(bias4[:, k * D:(k + 1) * D], bias.partition_broadcast(P)).then_inc(weights_loaded, 16)
            for u in range(1, RING):
                sp.dma_start(x_ring[u][:, :], unit_rows(x, u)).then_inc(x_loaded[u], 16)
            sp.wait_ge(blank, 5)
            for table, ap in ((dst_i, dst), (src_i, src), (w_l, edge_weight)):
                whole = ap[0:FULL * EPT].rearrange("(t c) -> t c", c=EPT)
                sp.dma_start(table[:, 0, 1:P], whole[0:P, :]).then_inc(edges_loaded, 16)
                sp.dma_start(table[0:FULL - P, 1, 1:P], whole[P:FULL, :]).then_inc(edges_loaded, 16)
                sp.dma_start(table[FULL - P:FULL - P + 1, 1, 1:1 + REST],
                             ap[FULL * EPT:E].rearrange("(o c) -> o c", o=1)).then_inc(edges_loaded, 16)
            whole = dst[0:FULL * EPT].rearrange("(t c) -> t c", c=EPT)
            sp.dma_start(dst_i[1:P, 0, 0:1], whole[0:P - 1, EPT - 1:EPT]).then_inc(edges_loaded, 16)
            sp.dma_start(dst_i[0:FULL - P + 1, 1, 0:1], whole[P - 1:FULL, EPT - 1:EPT]).then_inc(edges_loaded, 16)
            sp.dma_start(next_i[:, 0, 0:EPT], whole[0:P, :]).then_inc(edges_loaded, 16)
            sp.dma_start(next_i[0:FULL - P, 1, 0:EPT], whole[P:FULL, :]).then_inc(edges_loaded, 16)
            sp.dma_start(next_i[FULL - P:FULL - P + 1, 1, 0:REST],
                         dst[FULL * EPT:E].rearrange("(o c) -> o c", o=1)).then_inc(edges_loaded, 16)
            sp.dma_start(next_i[:, 0, EPT:P], whole[1:P + 1, 0:1]).then_inc(edges_loaded, 16)
            sp.dma_start(next_i[0:FULL - P - 1, 1, EPT:P], whole[P + 1:FULL, 0:1]).then_inc(edges_loaded, 16)
            sp.dma_start(next_i[FULL - P - 1:FULL - P, 1, EPT:P],
                         as_column(dst[FULL * EPT:FULL * EPT + 1])).then_inc(edges_loaded, 16)
            sp.dma_start(tail_of_node.rearrange("(p c) o -> p (c o)", p=P), absent).then_inc(table_blank, 16)
            sp.dma_start(list_dram.rearrange("(p c) f -> p (c f)", p=P), list_blank).then_inc(table_blank, 16)
            def load_unit(u, k):
                sp.wait_ge(xT_psum, 2 * u + 2)
                sp.dma_start(x_ring[k][:, :], unit_rows(x, u + RING)).then_inc(x_loaded[k], 16)

            def store_unit(u, k):
                sp.wait_ge(normed, u + 1)
                sp.dma_start(unit_rows(out, u), o_ring[k][:, :]).then_inc(stored[k], 16)

            def store_sums(c, g, slot, total):
                sp.wait_ge(sum_copied, total)
                sp.dma_start(c_dram[c][bass.ds(g * (G * P), G * P), :].rearrange("(k p) d -> p k d", p=P),
                             sums[slot][:, :, :]).then_inc(sums_stored[slot], 16)

            def blank_v(g):
                sp.dma_start(v_dram[bass.ds(g * (G * P), G * P), :].rearrange("(p r) d -> p (r d)", r=G),
                             bias4[:, :]).then_inc(v_blank, 16)

            def load_keys(g):
                until(sp, keys_loaded, 16 * g)
                sp.dma_start(keys_out[:, bass.ds(g * (G * P), G * P)],
                             keys_out_dram[bass.ds(g * (G * P), G * P)].partition_broadcast(P)).then_inc(keys_loaded, 16)

            def dense_unit(i, k):
                u = RING * i + k
                load_unit(u, k)
                if not isinstance(u, int) or u >= RING:
                    store_unit(u - RING, k)

            for k in range(RING):
                dense_unit(0, k)
            sp.wait_ge(floats_ready, 4)
            sp.dma_start(keys_out_dram.rearrange("(h p c) -> p h c", h=2, c=P), keys_f[:, :, :]).then_inc(keys_stored, 16)
            for k in range(RING):
                dense_unit(1, k)
            sp.wait_ge(keys_stored, 16)
            load_keys(0)
            with sp.Fori(2, A_START) as i:
                for k in range(RING):
                    dense_unit(i, k)

            def body_a(i, last):
                g = i - A_START
                for k in range(RING):
                    dense_unit(i, k)
                    if k == 0 and not last:
                        load_keys(g + 1)
                    if k == 1:
                        blank_v(g)
                store_sums(0, g, 0, G * g + G)

            with sp.Fori(A_START, B_START - 1) as i:
                body_a(i, False)
            body_a(B_START - 1, True)

            def body_b(i, last):
                stored_groups = 0
                for k in range(RING):
                    u = RING * i + k
                    if not last:
                        load_unit(u, k)
                    elif k == 0:
                        sp.wait_ge(xT_psum, 2 * u + 2)
                        sp.dma_start(x_ring[0][0:TAIL_P, 0:TAIL_RPP * D], tail_rows[0]).then_inc(x_loaded[0], 16)
                    store_unit(u - RING, k)
                    while G * stored_groups + G <= B_TILES[2 * k + 1].stop:
                        g = GB * (i - B_START) + stored_groups
                        store_sums(1, g, stored_groups, TILES + G * g + G)
                        stored_groups += 1

            with sp.Fori(B_START, BODIES - 1) as i:
                body_b(i, False)
            body_b(BODIES - 1, True)
            sp.wait_ge(table_done, 16 * TABLE_OPS * 3 * STEPS)
            sp.wait_ge(packed_blank, 1)
            rows = list_dram[0:TILES * EPT, :].rearrange("(t c) f -> t c f", c=EPT)
            sp.dma_start(packed[:, 0, 1:P, :], rows[0:P, :, :]).then_inc(packed_loaded, 16)
            sp.dma_start(packed[0:TILES - P, 1, 1:P, :], rows[P:TILES, :, :]).then_inc(packed_loaded, 16)
            sp.dma_start(packed[1:P, 0, 0, 0:1], rows[0:P - 1, EPT - 1, 0:1]).then_inc(packed_loaded, 16)
            sp.dma_start(packed[0:TILES - P, 1, 0, 0:1], rows[P - 1:TILES - 1, EPT - 1, 0:1]).then_inc(packed_loaded, 16)
            sp.dma_start(packed_next[:, 0:1], rows[1:P + 1, 0, 0:1]).then_inc(packed_loaded, 16)
            sp.dma_start(packed_next[0:TILES - P - 1, 1:2], rows[P + 1:TILES, 0, 0:1]).then_inc(packed_loaded, 16)
            for u in range(UNITS - RING, UNITS):
                store_unit(u, u % RING)
            sp.wait_ge(normed, UNITS + 1)
            sp.dma_start(tail_rows[1], o_ring[0][0:TAIL_P, 0:TAIL_RPP * D]).then_inc(stored[0], 16)
            for q in range(B_REST):
                g = B_BODIES * GB + q
                store_sums(1, g, q, TILES + G * g + G)

            sp.wait_ge(packed_floats, 1)
            sp.dma_start(keys_out2_dram.rearrange("(h p c) -> p h c", h=2, c=P), keys_f[:, :, :]).then_inc(keys2_stored, 16)
            sp.wait_ge(keys2_stored, 16)
            sp.wait_ge(sel_ready, AB_TILES)
            n_bodies = body_count(sp)

            def load_keys2(j):
                until(sp, keys2_loaded, 16 * j)
                sp.dma_start(keys_out[:, bass.ds(j * (CB * P), CB * P)],
                             keys_out2_dram[bass.ds(j * (CB * P), CB * P)].partition_broadcast(P)).then_inc(keys2_loaded, 16)

            load_keys2(0)
            with sp.Fori(1, n_bodies) as j:
                load_keys2(j)

            for k in range(GB):
                sp.wait_ge(sums_stored[k], 16 * ALL_STORES[k])
            for k in range(G):
                sp.wait_ge(v_scattered[k], n_bodies * (16 * CB // G))

            def body_d(j):
                for k in range(CB):
                    n = CB * j + k
                    until(sp, ta_psum, n - G + 1)
                    sp.dma_start(c1_in[k % G], c_dram[0][bass.ds(n * P, P), :]).then_inc(c1_loaded[k % G], 16)
                    until(sp, cy_copied, n - G + 1)
                    sp.dma_start(v_in[k % G], v_dram[bass.ds(n * P, P), :]).then_inc(v_loaded[k % G], 16)

            body_d(0)
            with sp.Fori(1, TILES // CB) as j:
                body_d(j)
            for k in range(RING):
                sp.wait_ge(stored[k], 16 * (BODIES + (k == 0)))
            for k in range(G):
                sp.wait_ge(scattered[k], 16 * GROUPS)

        @block.gpsimd
        def _(pool):
            pool.memset(ident[:, :], 0.0).then_inc(consts, 1)
            pool.wait_ge(consts, 1)
            pool.affine_select(out=ident[:, :], in_=ident[:, :], compare_op=ALU.not_equal, fill=1.0,
                               base=0, pattern=[[-1, P]], channel_multiplier=1).then_inc(identity_ready, 1)
            pool.iota(row_number[:, :], [[P, SLOTS]], base=0, channel_multiplier=1).then_inc(numbers_ready, 1)
            pool.iota(row_r[:, :, :], [[P * P, 2], [1, P]], base=0, channel_multiplier=P,
                      allow_small_or_imprecise_dtypes=True).then_inc(numbers_ready, 1)
            pool.iota(body_starts[:, :], [[CB * EPT, C_BODIES_MAX]], base=0, channel_multiplier=0,
                      allow_small_or_imprecise_dtypes=True).then_inc(numbers_ready, 1)
            pool.memset(ones[:, :], 1.0).then_inc(consts, 1)
            pool.memset(below[:, :], 1.0).then_inc(consts, 1)
            pool.memset(below_tile[:, :, :], 1.0).then_inc(consts, 1)
            pool.wait_ge(consts, 4)
            pool.affine_select(out=below[:, :], in_=below[:, :], compare_op=ALU.is_gt, fill=0.0,
                               base=0, pattern=[[1, P]], channel_multiplier=-1).then_inc(numbers_ready, 1)
            pool.affine_select(out=below_tile[:, :, :], in_=below_tile[:, :, :], compare_op=ALU.is_gt, fill=0.0,
                               base=0, pattern=[[-P, 2], [1, SLOTS]], channel_multiplier=-1).then_inc(numbers_ready, 1)
            nought = pool.alloc_register("nought")
            bound = pool.alloc_register("bound")
            pool.reg_mov(nought, 0)

            def limit(rows):
                pool.reg_add(bound, nought, rows - 1)

            def gather(dest, table, rows, index, s):
                pool.indirect_dma_start(dest, None, table, bass.IndirectOffsetOnAxis(ap=index, axis=0),
                                        bounds_check=bound, oob_is_err=False).then_inc(s, 16)

            def scatter(table, source, index, s):
                pool.indirect_dma_start(table, bass.IndirectOffsetOnAxis(ap=index, axis=0), source, None,
                                        bounds_check=bound, oob_is_err=False).then_inc(s, 16)

            def gather_group(g, slot, table, rows):
                pool.wait_ge(gather_staged, g + 1)
                limit(rows)
                for k in range(G):
                    if not isinstance(g, int) or g > 0:
                        pool.wait_ge(summed, G * g - G + k + 1)
                        limit(rows)
                    gather(rows_in[k][:, :], table, rows, gather_idx[slot][:, k:k + 1], gathered[k])

            def table_ops(i, step, ops):
                if ops[0] == 0:
                    pool.wait_ge(table_staged, i - A_START + 1)
                limit(TILES * EPT if step == "pack" else N)
                for k in ops:
                    if step == "enter":
                        scatter(tail_of_node[0:N, :], table_val[:, k:k + 1], table_idx[:, k:k + 1], table_done)
                    elif step == "look up":
                        gather(found[:, k:k + 1], tail_of_node[0:N, :], N, table_idx[:, k:k + 1], table_done)
                    else:
                        scatter(list_dram[0:TILES * EPT, :], record[:, k, :], table_idx[:, k:k + 1], table_done)

            def body_a(i, step):
                gather_group(i - A_START, 0, x[:, :], N)
                table_ops(i, step, range(TABLE_OPS))

            pool.wait_ge(table_blank, 32)
            pool.wait_ge(blank, 6)
            body_a(A_START, "enter")
            with pool.Fori(A_START + 1, A_START + STEPS) as i:
                body_a(i, "enter")
            pool.wait_ge(table_done, 16 * TABLE_OPS * STEPS)
            limit(N)
            with pool.Fori(A_START + STEPS, LISTED) as i:
                body_a(i, "look up")
            with pool.Fori(LISTED, B_START) as i:
                body_a(i, "pack")
            pool.wait_ge(sums_stored[0], 16 * A_STORES[0])
            limit(CROWS)

            def body_b(i, pack):
                m = i - B_START
                for k in range(GB):
                    gather_group(GROUPS + GB * m + k, k, c_dram[0][:, :], CROWS)
                    if pack:
                        table_ops(i, "pack", range(TABLE_OPS * k // GB, TABLE_OPS * (k + 1) // GB))

            with pool.Fori(B_START, LIST_END) as i:
                body_b(i, True)
            with pool.Fori(LIST_END, BODIES) as i:
                body_b(i, False)
            for k in range(B_REST):
                gather_group(GROUPS + B_BODIES * GB + k, k, c_dram[0][:, :], CROWS)

            for k in range(GB):
                pool.wait_ge(sums_stored[k], 16 * ALL_STORES[k])
            pool.wait_ge(v_blank, 16 * GROUPS)
            pool.wait_ge(normed, UNITS + 1)
            for k in range(RING):
                pool.wait_ge(stored[k], 16 * (BODIES + (k == 0)))
            n_bodies = body_count(pool)
            LAG = 6

            def scatter_v(n, group, late):
                pool.wait_ge(v_copied, n + 1)
                limit(CROWS)
                pool.wait_ge(v_staged, group + 1)
                limit(CROWS)
                scatter(v_dram[:, :], v_out[late % G], tailo_idx[late // G][:, late % G:late % G + 1],
                        v_scattered[late % G])

            def body_c(j):
                for k in range(CB):
                    n = CB * j + k
                    if k % G == 0:
                        pool.wait_ge(gather_staged, AB_GROUPS + 2 * j + k // G + 1)
                        limit(CROWS)
                    pool.wait_ge(summed, AB_TILES + n - G + 1)
                    limit(CROWS)
                    gather(rows_in[k % G][:, :], c_dram[1][:, :], CROWS, gather_idx[k // G][:, k % G:k % G + 1],
                           gathered[k % G])
                    until(pool, t_psum, n - G + 1)
                    limit(CROWS)
                    gather(own_c2[k % G], c_dram[1][:, :], CROWS, tailx_idx[k // G][:, k % G:k % G + 1],
                           own_gathered[k % G])
                    if not isinstance(j, int) or k >= LAG:
                        scatter_v(n - LAG, 2 * j + (k - LAG) // G, (k - LAG) % CB)

            body_c(0)
            with pool.Fori(1, n_bodies) as j:
                body_c(j)
            for k in range(CB - LAG, CB):
                scatter_v(CB * n_bodies - CB + k, 2 * n_bodies - 2 + k // G, k)

            def scatter_out(n, group, late):
                pool.wait_ge(cnormed, n + 1)
                limit(N)
                pool.wait_ge(tailo_staged, group + 1)
                limit(N)
                scatter(out[:, :], co[late % G], tailo_idx[late // G][:, late % G:late % G + 1], scattered[late % G])

            def body_d(j):
                for k in range(CB):
                    n = CB * j + k
                    if k % G == 0:
                        pool.wait_ge(tailx_staged, 2 * j + k // G + 1)
                        limit(N)
                    until(pool, ta_psum, n - G + 1)
                    limit(N)
                    gather(tail_x[k % G], x[:, :], N, tailx_idx[k // G][:, k % G:k % G + 1], tailx_in[k % G])
                    if not isinstance(j, int) or k >= LAG:
                        scatter_out(n - LAG, 2 * j + (k - LAG) // G, (k - LAG) % CB)

            body_d(0)
            with pool.Fori(1, TILES // CB) as j:
                body_d(j)
            for n in range(TILES - LAG, TILES):
                scatter_out(n, n // G, n % CB)

        @block.scalar
        def _(act):
            def copy_xT(p, k, rows=P):
                act.wait_ge(xT_psum, p + 1)
                until(act, y_psum, p - 1)
                view = [t[:, :].rearrange("p (q c) -> p q c", c=P)[:, :, 0:rows] for t in (xT[k % 2], ps_xT[k % 2])]
                act.copy(view[0], view[1]).then_inc(xT_copied, 1)

            def roots(u, slot, rows=P, tiles=RPP):
                act.wait_ge(var_ready, u + 1)
                act.activation(std[slot][0:rows, 0:tiles], mean_var[slot][0:rows, 0:tiles, 1], ACT.Sqrt,
                               bias=eps[0:rows, :]).then_inc(std_ready, 1)

            def normalise(u, slot, turn, half, rows=P):
                if half == 0:
                    act.wait_ge(shift_ready, u + 1)
                    until(act, stored[slot], 16 * turn)
                for r in (2 * half, 2 * half + 1):
                    last = act.activation(o_ring[slot][0:rows, r * D:(r + 1) * D], y_ring[slot][0:rows, r * D:(r + 1) * D],
                                          ACT.Identity, bias=shift[slot][0:rows, r:r + 1],
                                          scale=rstd[slot][0:rows, r:r + 1])
                if half == 1 or rows < P:
                    last.then_inc(normed, 1)

            def await_sum(e, carried):
                if carried:
                    act.wait_ge(carry_ready, e + 2)
                else:
                    act.wait_ge(summed, e + 1)

            def copy_sum(e, k, slot, uses, carried):
                await_sum(e, carried)
                if k == 0:
                    until(act, sums_stored[slot], 16 * uses)
                act.copy(sums[slot][:, k, :], ps_sum[k % 2][:, 0:D]).then_inc(sum_copied, 1)

            def pair(i, k):
                u, slot, half = RING * i + k // 2, k // 2, k % 2
                copy_xT(2 * RING * i + k, half)
                if half == 0 and (not isinstance(u, int) or u >= 3):
                    normalise(u - 3, slot, i - 1, 1)
                if half == 1 and (not isinstance(u, int) or u >= 1):
                    roots(u - 1, (slot - 1) % RING)
                if half == 1 and (not isinstance(u, int) or u >= 2):
                    normalise(u - 2, (slot - 2) % RING, i - (slot < 2), 0)

            act.wait_ge(blank, 6)
            for i in range(2):
                for k in range(2 * RING):
                    pair(i, k)
            for k in range(2 * RING):
                pair(2, k)

            def body_a(i):
                g = i - A_START
                for k in range(2 * RING):
                    pair(i, k)
                    if k >= 2:
                        copy_sum(G * g + k - 2, k - 2, 0, g, k < G + 1)

            body_a(A_START)
            with act.Fori(A_START + 1, B_START) as i:
                body_a(i)

            def body_b(i):
                m = i - B_START
                for k in range(2 * RING):
                    for q in B_TILES[k]:
                        if q == B_TILES[k].start + 1:
                            pair(i, k)
                        copy_sum(TILES + GB * G * m + q, q % G, q // G, A_STORES[q // G] + m, True)

            body_b(B_START)
            with act.Fori(B_START + 1, BODIES) as i:
                body_b(i)
            copy_xT(2 * UNITS, 0, TAIL_P)
            normalise(UNITS - 3, 0, BODIES - 1, 1)
            roots(UNITS - 1, 2)
            normalise(UNITS - 2, 1, BODIES - 1, 0)
            normalise(UNITS - 2, 1, BODIES - 1, 1)
            roots(UNITS, 0, TAIL_P, TAIL_RPP)
            normalise(UNITS - 1, 2, BODIES - 1, 0)
            normalise(UNITS - 1, 2, BODIES - 1, 1)
            normalise(UNITS, 0, BODIES, 0, TAIL_P)

            for q in range(B_REST * G):
                copy_sum(TILES + GB * G * B_BODIES + q, q % G, q // G, A_STORES[q // G] + B_BODIES, q < B_REST * G - 1)

            for k in range(GB):
                act.wait_ge(sums_stored[k], 16 * ALL_STORES[k])
            n_bodies = body_count(act)

            def body_c(j):
                for k in range(CB):
                    n = CB * j + k
                    await_sum(AB_TILES + n, k < CB - 1)
                    until(act, t_psum, n - G + 1)
                    act.copy(sums[0][:, k % G, :], ps_sum[k % 2][:, 0:D]).then_inc(sum_copied, 1)
                    act.wait_ge(t_psum, n + 1)
                    until(act, v_psum, n - 1)
                    act.copy(xT[k % 2][:, :], ps_xT[k % 2][:, :]).then_inc(t_copied, 1)

            body_c(0)
            with act.Fori(1, n_bodies) as j:
                body_c(j)

            act.wait_ge(normed, UNITS + 1)
            act.wait_ge(v_psum, n_bodies * CB)

            def c_roots(n, k):
                act.wait_ge(cvar_ready, n + 1)
                act.activation(cstd[k % G][:, :], cmv[k % G][:, 1:2], ACT.Sqrt, bias=eps[:, :]).then_inc(cstd_ready, 1)

            def c_normalise(n, k, turn):
                act.wait_ge(cshift_ready, n + 1)
                until(act, scattered[k % G], 16 * turn)
                act.activation(co[k % G], cy[k % G], ACT.Identity, bias=cshift[k % G][:, :],
                               scale=crstd[k % G][:, :]).then_inc(cnormed, 1)

            def d_tile(n, j, k):
                act.wait_ge(ta_psum, n + 1)
                until(act, cy_psum, n - 1)
                act.copy(xT[k % 2][:, :], ps_xT[k % 2][:, :]).then_inc(ta_copied, 1)
                if not isinstance(n, int) or n >= 2:
                    c_roots(n - 2, (k - 2) % G)
                if not isinstance(n, int) or n >= 3:
                    c_normalise(n - 3, (k - 3) % G, j - (k < 3))

            for n in range(2 * G):
                d_tile(n, n // G, n % G)
            with act.Fori(2, GROUPS) as j:
                for k in range(G):
                    d_tile(G * j + k, j, k)
            c_roots(TILES - 2, (TILES - 2) % G)
            c_normalise(TILES - 3, (TILES - 3) % G, GROUPS - 1)
            c_roots(TILES - 1, (TILES - 1) % G)
            c_normalise(TILES - 2, (TILES - 2) % G, GROUPS - 1)
            c_normalise(TILES - 1, (TILES - 1) % G, GROUPS - 1)

        @block.tensor
        def _(pe):
            pe.wait_ge(identity_ready, 1)
            pe.wait_ge(w0_ready, KC)

            def turn_pair(p, k, i, rows=P):
                slot, half = k // 2, k % 2
                if half == 0:
                    pe.wait_ge(x_loaded[slot], 16 * i + 16)
                until(pe, xT_copied, p - 1)
                for r in range(2):
                    for c in range(KC):
                        at = (2 * half + r) * D + c * P
                        q = r * KC + c
                        last = pe.transpose(ps_xT[half][:, q * P:q * P + rows], x_ring[slot][0:rows, at:at + P],
                                            ident[0:rows, 0:rows])
                return last.then_inc(xT_psum, 1)

            def multiply_pair(p, half, tiles=(0, 1), rows=P):
                if tiles[0] == 0:
                    pe.wait_ge(xT_copied, p + 1)
                    until(pe, y_copied, p - 1)
                for r in tiles:
                    for c in range(KC):
                        q = r * KC + c
                        last = pe.matmul(ps_y[half][0:rows, r * D:(r + 1) * D], xT[half][:, q * P:q * P + rows],
                                         w_sb[:, c, :], start=c == 0, stop=c == KC - 1)
                if tiles[-1] == 1:
                    last.then_inc(y_psum, 1)

            def sum_tile(e, k):
                pe.wait_ge(sel_ready, e + 1)
                pe.wait_ge(carry_ready, e + 1)
                until(pe, sum_copied, e - 1)
                pe.matmul(ps_sum[k % 2][:, 0:D], sel[k % G][:, :], rows_in[k % G][:, :],
                          start=True, stop=True).then_inc(summed, 1)

            def body_a(i, tiles):
                for k in range(2 * RING):
                    p = 2 * RING * i + k
                    turn_pair(p, k, i)
                    if not isinstance(p, int) or p >= 1:
                        multiply_pair(p - 1, (k - 1) % 2)
                    if tiles and k >= 2:
                        sum_tile(G * (i - A_START) + k - 2, k - 2)

            def body_b(i, first):
                for k in range(2 * RING):
                    p = 2 * RING * i + k
                    tiles = [(TILES + GB * G * (i - B_START) + q, q % G) for q in B_TILES[k]]
                    turn_pair(p, k, i)
                    sum_tile(*tiles[0])
                    if k or not first:
                        multiply_pair(p - 1, (k - 1) % 2, (0,))
                    sum_tile(*tiles[1])
                    if k or not first:
                        multiply_pair(p - 1, (k - 1) % 2, (1,))
                    for tile in tiles[2:]:
                        sum_tile(*tile)

            def turn_lists(lists, done):
                for q, rows in enumerate(lists):
                    for h in range(2):
                        at = (2 * (q % 2) + h) * P
                        last = pe.transpose(ps_list[q // 2][:, at:at + P], rows[h], ident[:, :])
                last.then_inc(done, 1)

            body_a(0, False)
            pe.wait_ge(floats_ready, 4)
            turn_lists([[t[:, h, :] for h in range(2)] for t in (dst_f, next_f, src_f, w_l)], lists_turned)
            body_a(1, False)
            pe.wait_ge(tables_ready, 2)
            turn_lists([[own_r[:, h, :] for h in range(2)]], own_turned)
            pe.wait_ge(later_ready, 1)
            pe.matmul(ps_list[1][:, 0:SLOTS], ones[0:1, :], later[:, :], start=True, stop=True).then_inc(later_spread, 1)
            body_a(2, False)
            body_a(A_START, True)
            with pe.Fori(A_START + 1, LISTED) as i:
                body_a(i, True)
            pe.wait_ge(active_ready, 1)
            pe.matmul(ps_list[0][:, 0:SLOTS], below[:, :], active[:, :], start=True, stop=True)
            for h in range(2):
                last = pe.matmul(ps_list[1][:, h:h + 1], active[:, h * P:(h + 1) * P], ones[:, 0:1], start=True, stop=True)
            last.then_inc(counted, 1)
            pe.wait_ge(totals_ready, 1)
            for h in range(2):
                last = pe.matmul(ps_list[1][:, SLOTS:2 * SLOTS], totals_bc[:, h, :], below_tile[:, h, :],
                                 start=h == 0, stop=h == 1)
            last.then_inc(based, 1)
            with pe.Fori(LISTED, B_START) as i:
                body_a(i, True)
            multiply_pair(2 * RING * B_START - 1, 1)
            body_b(B_START, True)
            with pe.Fori(B_START + 1, BODIES) as i:
                body_b(i, False)
            turn_pair(2 * UNITS, 0, BODIES, TAIL_P)
            multiply_pair(2 * UNITS - 1, 1)
            multiply_pair(2 * UNITS, 0, rows=TAIL_P)
            for q in range(B_REST * G):
                sum_tile(TILES + GB * G * B_BODIES + q, q % G)
            pe.wait_ge(packed_floats, 3)
            turn_lists([[packed[:, h, :, f] for h in range(2)] for f in range(3)]
                       + [[own_r[:, h, :] for h in range(2)]], packed_turned)

            n_bodies = body_count(pe)
            pe.wait_ge(xT_copied, PAIRS)
            pe.wait_ge(y_copied, PAIRS)

            def turn_rows(banks, rows, done):
                for r, part in enumerate(rows):
                    for c in range(KC):
                        q = r * KC + c
                        last = pe.transpose(banks[:, q * P:(q + 1) * P], part[:, c * P:(c + 1) * P], ident[:, :])
                last.then_inc(done, 1)

            def multiply(k, first, done):
                for q in range(2 * KC):
                    last = pe.matmul(ps_y[k % 2][:, 0:D], xT[k % 2][:, q * P:(q + 1) * P], w_sb[:, first + q, :],
                                     start=q == 0, stop=q == 2 * KC - 1)
                last.then_inc(done, 1)

            def multiply_v(n, k):
                pe.wait_ge(t_copied, n + 1)
                until(pe, v_copied, n - 1)
                multiply(k, 2 * KC, v_psum)

            def body_c(j):
                for k in range(CB):
                    n = CB * j + k
                    sum_tile(AB_TILES + n, k)
                    if not isinstance(n, int) or n > 0:
                        multiply_v(n - 1, k - 1)
                    pe.wait_ge(own_gathered[k % G], 32 * j + 16 * (k // G) + 16)
                    pe.wait_ge(sum_copied, AB_TILES + n + 1)
                    until(pe, t_copied, n - 1)
                    turn_rows(ps_xT[k % 2], (own_c2[k % G], sums[0][:, k % G, :]), t_psum)

            body_c(0)
            with pe.Fori(1, n_bodies) as j:
                body_c(j)
            multiply_v(CB * n_bodies - 1, CB - 1)

            pe.wait_ge(t_copied, CB * n_bodies)
            pe.wait_ge(v_copied, CB * n_bodies)

            def multiply_d(n, k):
                pe.wait_ge(ta_copied, n + 1)
                until(pe, cy_copied, n - 1)
                multiply(k, 0, cy_psum)

            def body_d(j):
                for k in range(G):
                    n = G * j + k
                    pe.wait_ge(tailx_in[k], 16 * j + 16)
                    pe.wait_ge(c1_loaded[k], 16 * j + 16)
                    until(pe, ta_copied, n - 1)
                    turn_rows(ps_xT[k % 2], (tail_x[k], c1_in[k]), ta_psum)
                    if not isinstance(n, int) or n > 0:
                        multiply_d(n - 1, k - 1)

            body_d(0)
            with pe.Fori(1, GROUPS) as j:
                body_d(j)
            multiply_d(TILES - 1, TILES - 1)

        @block.vector
        def _(dve):
            dve.memset(dst_i[:, :, :], -1).then_inc(blank, 1)
            dve.memset(next_i[:, :, :], -1).then_inc(blank, 1)
            dve.memset(src_i[:, :, :], ABSENT).then_inc(blank, 1)
            dve.memset(absent, ABSENT)
            blank_fields = list_blank.rearrange("p (c f) -> p c f", f=FIELDS)
            for f, value in enumerate((-1.0, 0.0, float(ABSENT), float(ABSENT))):
                last = dve.memset(blank_fields[:, :, f], value)
            last.then_inc(blank, 1)
            dve.memset(w_l[:, :, 1:P], 0.0)
            dve.memset(w_l[:, :, 0:1], 1.0).then_inc(blank, 1)
            dve.memset(found[:, :], ABSENT)
            dve.memset(src_tail[:, :], ABSENT)
            for k in range(G):
                dve.memset(rows_in[k][:, :], 0.0)
            dve.memset(eps[:, :], EPS).then_inc(blank, 1)
            dve.wait_ge(weights_loaded, 16 * (1 + RPP))
            dve.wait_ge(identity_ready, 1)
            for c in range(KC):
                dve.tensor_tensor(w_sb[:, c, c * P:(c + 1) * P], w_sb[:, c, c * P:(c + 1) * P], ident[:, :],
                                  ALU.add).then_inc(w0_ready, 1)
            def columns(dest, table, t, n):
                return dve.tensor_scalar(dest, table[:, bass.ds(t, n)], 0, None, ALU.add)

            def copy_y(p, u, slot, half, rows=P):
                dve.wait_ge(y_psum, p + 1)
                until(dve, normed, u - RING + 1)
                dve.tensor_tensor(y_ring[slot][0:rows, half * 2 * D:(half + 1) * 2 * D], ps_y[half][0:rows, :],
                                  bias2[0:rows, :], ALU.add).then_inc(y_copied, 1)

            def unit_stats(p, slot, half, rows=P):
                dve.wait_ge(y_copied, p + 1)
                for r in (2 * half, 2 * half + 1):
                    last = dve.bn_stats(stats[slot][0:rows, r, :], y_ring[slot][0:rows, r * D:(r + 1) * D])
                last.then_inc(stats_ready, 1)

            def unit_inverse(u, slot, rows=P, tiles=RPP):
                dve.wait_ge(std_ready, u + 1)
                dve.reciprocal(rstd[slot][0:rows, 0:tiles], std[slot][0:rows, 0:tiles]).then_inc(rstd_ready, 1)

            def unit_variance(slot, rows=P, tiles=RPP):
                for r in range(tiles):
                    last = dve.bn_aggr(mean_var[slot][0:rows, r, :], stats[slot][0:rows, r, :])
                last.then_inc(var_ready, 1)

            def unit_shift(u, slot, rows=P, tiles=RPP):
                dve.wait_ge(rstd_ready, u + 1)
                dve.scalar_tensor_tensor(out=shift[slot][0:rows, 0:tiles], in0=mean_var[slot][0:rows, 0:tiles, 0],
                                         scalar=-1.0, in1=rstd[slot][0:rows, 0:tiles], op0=ALU.mult,
                                         op1=ALU.mult).then_inc(shift_ready, 1)

            def unit_end(u, k):
                dve.wait_ge(stats_ready, 2 * u + 2)
                if not isinstance(u, int) or u >= 1:
                    unit_inverse(u - 1, (k - 1) % RING)
                unit_variance(k)
                if not isinstance(u, int) or u >= 1:
                    unit_shift(u - 1, (k - 1) % RING)

            def select(e, k, t, weights, keys=key_in):
                until(dve, summed, e - G + 1)
                dve.tensor_scalar(sel[k % G][:, :], keys_out[:, bass.ds(t * P, P)], keys[:, bass.ds(t, 1)],
                                  weights[:, bass.ds(t, 1)], ALU.is_equal, ALU.mult).then_inc(sel_ready, 1)

            def carry_of(e, g, k, before):
                dve.wait_ge(gathered[k], 16 * g + 16)
                if before is None:
                    dve.memset(rows_in[k][0:1, :], 0.0).then_inc(carry_ready, 1)
                elif before == "psum":
                    dve.wait_ge(summed, e)
                    dve.tensor_copy(rows_in[k][0:1, :], ps_sum[(k - 1) % 2][0:1, 0:D]).then_inc(carry_ready, 1)
                else:
                    dve.wait_ge(sum_copied, e)
                    dve.tensor_copy(rows_in[k][0:1, :], sums[0][0:1, G - 1, :]).then_inc(carry_ready, 1)

            def stage_table(i, step):
                until(dve, table_done, 16 * TABLE_OPS * i)
                if step == "enter":
                    columns(table_idx[:, :], tail_node, TABLE_OPS * i, TABLE_OPS)
                    columns(table_val[:, :], row_number, TABLE_OPS * i, TABLE_OPS).then_inc(table_staged, 1)
                elif step == "look up":
                    if not isinstance(i, int) or i > STEPS:
                        columns_found(i - STEPS - 1)
                    columns(table_idx[:, :], src_node, TABLE_OPS * (i - STEPS), TABLE_OPS).then_inc(table_staged, 1)
                else:
                    t = TABLE_OPS * (i - 2 * STEPS)
                    for f, table in enumerate((key_in, w1, src_tail, own)):
                        columns(record[:, :, f], table, t, TABLE_OPS)
                    columns(table_idx[:, :], place, t, TABLE_OPS).then_inc(table_staged, 1)

            def columns_found(q):
                dve.tensor_scalar(src_tail[:, bass.ds(TABLE_OPS * q, TABLE_OPS)], found[:, :], 0, None,
                                  ALU.add).then_inc(found_copied, 1)

            def copy_pair(i, k):
                copy_y(2 * RING * i + k, RING * i + k // 2, k // 2, k % 2)

            def measure_pair(i, k):
                u, slot, half = RING * i + k // 2, k // 2, k % 2
                unit_stats(2 * RING * i + k, slot, half)
                if half:
                    unit_end(u, slot)

            def dense_body(i, pairs=range(2 * RING)):
                for k in pairs:
                    copy_pair(i, k)
                    measure_pair(i, k)

            def body_a(i, step, last=False, before_last_pair=None):
                g = i - A_START
                e = G * g
                copy_pair(i, 0)
                stage_table(g, step)
                measure_pair(i, 0)
                dve.wait_ge(keys_loaded, 16 * g + 16)
                for k in range(G):
                    select(e + k, k, G * g + k, w1)
                carry_of(e, g, 0, None if isinstance(e, int) and e == 0 else "sums")
                for k in range(G):
                    copy_pair(i, k + 1)
                    if k + 1 < G:
                        carry_of(e + k + 1, g, k + 1, "psum")
                    elif not last:
                        columns(gather_idx[0][:, :], src_node, G * g + G, G).then_inc(gather_staged, 1)
                    measure_pair(i, k + 1)
                if before_last_pair is not None:
                    before_last_pair()
                copy_pair(i, G + 1)
                measure_pair(i, G + 1)

            dense_body(0, range(2 * RING - 1))
            dve.wait_ge(edges_loaded, 16 * 17)
            dve.tensor_copy(dst_f[:, :, :], dst_i[:, :, :]).then_inc(floats_ready, 1)
            dve.tensor_copy(next_f[:, :, :], next_i[:, :, :]).then_inc(floats_ready, 1)
            dve.tensor_copy(src_f[:, :, :], src_i[:, :, :]).then_inc(floats_ready, 1)
            dve.tensor_copy(keys_f[:, :, 1:P], dst_i[:, :, 1:P])
            dve.tensor_copy(keys_f[:, :, 0:1], dst_i[:, :, P - 1:P]).then_inc(floats_ready, 1)
            dve.wait_ge(lists_turned, 1)
            dve.tensor_copy(key_in[:, :], ps_list[0][:, 0:SLOTS]).then_inc(table_chain, 1)
            dve.tensor_copy(src_node[:, :], ps_list[1][:, 0:SLOTS])
            dve.tensor_copy(w1[:, :], ps_list[1][:, SLOTS:2 * SLOTS])
            dve.wait_ge(table_chain, 1)
            dve.tensor_tensor(tail_f[:, :], key_in[:, :], ps_list[0][:, SLOTS:2 * SLOTS],
                              ALU.is_equal).then_inc(table_chain, 1)
            dve.wait_ge(table_chain, 2)
            dve.scalar_tensor_tensor(out=tail_node[:, :], in0=tail_f[:, :], scalar=float(ABSENT), in1=key_in[:, :],
                                     op0=ALU.mult, op1=ALU.add).then_inc(table_chain, 1)
            dve.wait_ge(table_chain, 3)
            dve.memset(tail_node[0:1, :], ABSENT).then_inc(tables_ready, 1)
            dve.tensor_scalar(not_padding[:, :], src_node[:, :], N, None, ALU.is_lt)
            dve.wait_ge(numbers_ready, 5)

            steps_done = [0]

            def after(instruction, s, count):
                count[0] += 1
                instruction.then_inc(s, 1)
                dve.wait_ge(s, count[0])

            after(dve.tensor_tensor(own_r[:, :, :], dst_f[:, :, :], next_f[:, :, :], ALU.is_equal), own_chain, steps_done)
            after(dve.scalar_tensor_tensor(out=own_r[:, :, :], in0=own_r[:, :, :], scalar=float(ABSENT),
                                           in1=row_r[:, :, :], op0=ALU.mult, op1=ALU.add), own_chain, steps_done)
            after(dve.memset(own_r[:, :, 0:1], float(ABSENT)), own_chain, steps_done)
            for d in (1, 2, 4, 8, 16, 32, 64):
                after(dve.tensor_tensor(own_r[:, :, 0:P - d], own_r[:, :, 0:P - d], own_r[:, :, d:P], ALU.min),
                      own_chain, steps_done)
            dve.memset(later[:, :], float(ABSENT)).then_inc(tables_ready, 1)
            columns(gather_idx[0][:, :], src_node, 0, G).then_inc(gather_staged, 1)
            dense_body(0, range(2 * RING - 1, 2 * RING))
            dense_body(1, range(2 * RING - 1))
            dve.wait_ge(own_turned, 1)
            after(dve.tensor_copy(own_T[:, :], ps_list[0][:, 0:SLOTS]), own_chain, steps_done)
            after(dve.tensor_copy(later[:, 0:SLOTS - 1], own_T[0:1, 1:SLOTS]), own_chain, steps_done)
            for d in (1, 2, 4, 8, 16, 32, 64, 128):
                after(dve.tensor_tensor(later[:, 0:SLOTS - d], later[:, 0:SLOTS - d], later[:, d:SLOTS], ALU.min),
                      own_chain, steps_done)
            dve.memset(inactive[:, :], 0.0).then_inc(later_ready, 1)
            dve.wait_ge(later_spread, 1)
            after(dve.tensor_tensor(own[:, :], own_T[:, :], ps_list[1][:, 0:SLOTS], ALU.min), own_chain, steps_done)
            dense_body(1, range(2 * RING - 1, 2 * RING))
            dense_body(2)

            def find_places():
                dve.wait_ge(table_done, 16 * TABLE_OPS * 2 * STEPS)
                columns_found(STEPS - 1)
                dve.wait_ge(found_copied, STEPS)
                dve.scalar_tensor_tensor(out=active[:, :], in0=src_tail[:, :], scalar=float(CROWS),
                                         in1=not_padding[:, :], op0=ALU.is_lt, op1=ALU.mult).then_inc(active_ready, 1)
                dve.wait_ge(active_ready, 1)
                done = [0]
                after(dve.tensor_tensor(w2[:, :], w1[:, :], active[:, :], ALU.mult), w2_ready, [0])
                dve.memset(w2[0:1, :], 1.0).then_inc(w2_ready, 1)
                after(dve.tensor_scalar(inactive[:, :], active[:, :], -float(ABSENT), float(ABSENT), ALU.mult, ALU.add),
                      place_chain, done)
                dve.wait_ge(counted, 1)
                after(dve.tensor_copy(totals[:, :], ps_list[1][:, 0:2]), place_chain, done)
                for h in range(2):
                    last = dve.tensor_scalar(totals_bc[:, h, :], ones[:, :], totals[:, h:h + 1], None, ALU.mult)
                last.then_inc(totals_ready, 1)
                after(dve.tensor_tensor(place_f[:, :], inactive[:, :], ps_list[0][:, 0:SLOTS], ALU.add), place_chain, done)
                dve.wait_ge(based, 1)
                after(dve.tensor_tensor(place[:, :], place_f[:, :], ps_list[1][:, SLOTS:2 * SLOTS], ALU.add),
                      place_chain, done)
                after(dve.tensor_copy(total[:, :], ps_list[1][0:1, SLOTS + TILES:SLOTS + TILES + 1]), place_chain, done)
                after(dve.tensor_scalar(started[:, :], body_starts[:, :], total[:, :], None, ALU.is_lt), place_chain, done)
                after(dve.reduce_sum(bodies_f[:, :], started[:, :], mybir.AxisListType.X), place_chain, done)
                dve.tensor_scalar(more_bodies[:, :], bodies_f[:, :], -2.0, 0.0, ALU.add, ALU.max).then_inc(bodies_ready, 1)

            body_a(A_START, "enter")
            with dve.Fori(A_START + 1, A_START + STEPS) as i:
                body_a(i, "enter")
            body_a(A_START + STEPS, "look up")
            with dve.Fori(A_START + STEPS + 1, LISTED - 1) as i:
                body_a(i, "look up")
            body_a(LISTED - 1, "look up", before_last_pair=find_places)
            with dve.Fori(LISTED, B_START - 1) as i:
                body_a(i, "pack")
            body_a(B_START - 1, "pack", last=True)

            dve.wait_ge(w2_ready, 2)
            columns(gather_idx[0][:, :], src_tail, 0, G).then_inc(gather_staged, 1)
            select(TILES, 0, 0, w2)
            select(TILES + 1, 1, 1, w2)
            carry_of(TILES, GROUPS, 0, None)

            def tile_b(m, q, left=GB * G):
                e, t = TILES + GB * G * m + q, GB * G * m + q
                if q % G == 0 and q + G < left or left == GB * G and q % G == 0:
                    columns(gather_idx[(q // G + 1) % GB][:, :], src_tail, t + G, G).then_inc(gather_staged, 1)
                if q + 1 < left or left == GB * G:
                    carry_of(e + 1, GROUPS + GB * m + (q + 1) // G, (q + 1) % G, "psum")
                if q + 2 < left or left == GB * G:
                    select(e + 2, q + 2, t + 2, w2)

            def body_b(i, first, pack):
                m = i - B_START
                for k in range(2 * RING):
                    tiles = list(B_TILES[k])
                    dense = not (first and k == 0)
                    before = (i, k - 1) if k else (i - 1, 2 * RING - 1)
                    tile_b(m, tiles[0])
                    if k == 0 and pack:
                        stage_table(i - A_START, "pack")
                    tile_b(m, tiles[1])
                    if dense:
                        copy_pair(*before)
                    for q in tiles[2:]:
                        tile_b(m, q)
                    if dense:
                        measure_pair(*before)

            body_b(B_START, True, True)
            with dve.Fori(B_START + 1, LIST_END) as i:
                body_b(i, False, True)
            with dve.Fori(LIST_END, BODIES) as i:
                body_b(i, False, False)
            dve.wait_ge(xT_psum, 2 * UNITS - 2)
            dve.memset(packed[:, :, 1:P, :], 0.0)
            dve.memset(packed[:, :, 0, 0], -1.0)
            dve.memset(packed[:, :, 0, 1], 1.0)
            dve.memset(packed[:, :, 0, 2:FIELDS], float(ABSENT))
            dve.memset(packed_next[:, :], -1.0).then_inc(packed_blank, 1)
            copy_pair(BODIES - 1, 2 * RING - 1)
            measure_pair(BODIES - 1, 2 * RING - 1)
            copy_y(2 * UNITS, UNITS, 0, 0, TAIL_P)
            unit_stats(2 * UNITS, 0, 0, TAIL_P)
            dve.wait_ge(stats_ready, 2 * UNITS + 1)
            unit_inverse(UNITS - 1, RING - 1)
            unit_variance(0, TAIL_P, TAIL_RPP)
            unit_shift(UNITS - 1, RING - 1)
            unit_inverse(UNITS, 0, TAIL_P, TAIL_RPP)
            unit_shift(UNITS, 0, TAIL_P, TAIL_RPP)
            for q in range(B_REST * G):
                tile_b(B_BODIES, q, B_REST * G)
            dve.wait_ge(packed_loaded, 16 * 6)
            dve.wait_ge(keys_stored, 16)
            dve.tensor_copy(keys_f[:, :, 1:P], packed[:, :, 1:P, 0])
            dve.tensor_copy(keys_f[:, :, 0:1], packed[:, :, P - 1:P, 0]).then_inc(packed_floats, 1)
            dve.tensor_tensor(own_r[:, :, 0:P - 1], packed[:, :, 0:P - 1, 0], packed[:, :, 1:P, 0], ALU.is_equal)
            after(dve.tensor_tensor(own_r[:, :, P - 1], packed[:, :, P - 1, 0], packed_next[:, :], ALU.is_equal),
                  own_chain, steps_done)
            after(dve.scalar_tensor_tensor(out=own_r[:, :, :], in0=own_r[:, :, :], scalar=float(ABSENT),
                                           in1=packed[:, :, :, 3], op0=ALU.mult, op1=ALU.add), own_chain, steps_done)
            dve.memset(own_r[:, :, 0:1], float(ABSENT)).then_inc(packed_floats, 2)
            dve.wait_ge(packed_turned, 1)
            dve.tensor_copy(key_in2[:, :], ps_list[0][:, 0:SLOTS])
            dve.tensor_copy(w_packed[:, :], ps_list[0][:, SLOTS:2 * SLOTS])
            dve.tensor_copy(src_tail2[:, :], ps_list[1][:, 0:SLOTS])
            dve.tensor_copy(own2[:, :], ps_list[1][:, SLOTS:2 * SLOTS]).then_inc(packed_tables, 1)
            dve.wait_ge(packed_tables, 1)

            n_bodies = body_count(dve)
            dve.wait_ge(normed, UNITS + 1)
            for k in range(RING):
                dve.wait_ge(stored[k], 16 * (BODIES + (k == 0)))

            def stage_c(g, half):
                columns(tailx_idx[half][:, :], own2, G * g, G)
                columns(gather_idx[half][:, :], src_tail2, G * g, G).then_inc(gather_staged, 1)

            def copy_v(n, k, turn):
                dve.wait_ge(v_psum, n + 1)
                until(dve, v_scattered[k % G], 16 * turn)
                dve.tensor_tensor(v_out[k % G], ps_y[k % 2][:, 0:D], bias4[:, 0:D], ALU.add).then_inc(v_copied, 1)

            def body_c(j):
                dve.wait_ge(keys2_loaded, 16 * j + 16)
                select(AB_TILES + CB * j, 0, CB * j, w_packed, key_in2)
                carry_of(AB_TILES + CB * j, AB_GROUPS + 2 * j, 0, None if isinstance(j, int) else "sums")
                select(AB_TILES + CB * j + 1, 1, CB * j + 1, w_packed, key_in2)
                for k in range(CB):
                    n, g = CB * j + k, 2 * j + k // G
                    if k % G == 0:
                        for q in range(G):
                            until(dve, own_gathered[q], 16 * g)
                        stage_c(g + 1, (k // G + 1) % 2)
                    if k + 1 < CB:
                        carry_of(AB_TILES + n + 1, AB_GROUPS + 2 * j + (k + 1) // G, (k + 1) % G, "psum")
                    if k + 2 < CB:
                        select(AB_TILES + n + 2, k + 2, n + 2, w_packed, key_in2)
                    if k % G == 1:
                        for q in range(G):
                            until(dve, v_scattered[q], 16 * (g - 1))
                        columns(tailo_idx[k // G][:, :], own2, G * g, G).then_inc(v_staged, 1)
                    if not isinstance(n, int) or n > 0:
                        copy_v(n - 1, k - 1, g - (k % G == 0))

            stage_c(0, 0)
            body_c(0)
            body_c(1)
            with dve.Fori(2, n_bodies) as j:
                body_c(j)
            copy_v(CB * n_bodies - 1, CB - 1, 2 * n_bodies - 1)

            for q in range(G):
                dve.wait_ge(own_gathered[q], n_bodies * (16 * CB // G))
                dve.wait_ge(v_scattered[q], n_bodies * (16 * CB // G))

            def stage_d(g, half):
                columns(tailx_idx[half][:, :], tail_node, G * g, G).then_inc(tailx_staged, 1)

            def c_copy(n, k, use):
                dve.wait_ge(cy_psum, n + 1)
                dve.wait_ge(v_loaded[k % G], 16 * use)
                until(dve, cnormed, n - G + 1)
                dve.tensor_tensor(cy[k % G], ps_y[k % 2][:, 0:D], v_in[k % G], ALU.add).then_inc(cy_copied, 1)
                dve.wait_ge(cy_copied, n + 1)
                dve.bn_stats(cstats[k % G][:, :], cy[k % G]).then_inc(cstats_ready, 1)

            def c_inverse(n, k):
                dve.wait_ge(cstd_ready, n + 1)
                dve.reciprocal(crstd[k % G][:, :], cstd[k % G][:, :]).then_inc(crstd_ready, 1)

            def c_variance(k):
                dve.bn_aggr(cmv[k % G][:, :], cstats[k % G][:, :]).then_inc(cvar_ready, 1)

            def c_shift(n, k):
                dve.wait_ge(crstd_ready, n + 1)
                dve.scalar_tensor_tensor(out=cshift[k % G][:, :], in0=cmv[k % G][:, 0:1], scalar=-1.0,
                                         in1=crstd[k % G][:, :], op0=ALU.mult, op1=ALU.mult).then_inc(cshift_ready, 1)

            def c_finish(n, k, use):
                if not isinstance(n, int) or n >= 1:
                    c_copy(n - 1, k - 1, use)
                    dve.wait_ge(cstats_ready, n)
                    if not isinstance(n, int) or n >= 2:
                        c_inverse(n - 2, k - 2)
                    c_variance(k - 1)
                    if not isinstance(n, int) or n >= 2:
                        c_shift(n - 2, k - 2)

            def body_d(j):
                for k in range(CB):
                    n, g = CB * j + k, 2 * j + k // G
                    if k % G == 0:
                        for q in range(G):
                            until(dve, tailx_in[q], 16 * g)
                        stage_d(g + 1, (k // G + 1) % 2)
                    if k % G == 1:
                        for q in range(G):
                            until(dve, scattered[q], 16 * (g - 1))
                        columns(tailo_idx[k // G][:, :], tail_node, G * g, G).then_inc(tailo_staged, 1)
                    c_finish(n, k, g + (k % G > 0))

            stage_d(0, 0)
            body_d(0)
            with dve.Fori(1, TILES // CB) as j:
                body_d(j)
            c_finish(TILES, TILES, GROUPS)
            c_inverse(TILES - 1, TILES - 1)
            c_shift(TILES - 1, TILES - 1)


_INS = ["x", "src", "dst", "edge_weight", "L0_gnn_shared_weight", "L0_gnn_output_bias"]


def kernel(**inputs):
    import numpy as _np
    import concourse.bacc as _bacc
    from concourse import mybir as _mybir
    from concourse.bass_utils import run_bass_kernel_spmd as _run

    nc = _bacc.Bacc("TRN2", target_bir_lowering=False, num_devices=1)
    arrays, args = {}, []
    for name in _INS:
        a = _np.ascontiguousarray(inputs[name])
        arrays[f"in_{name}"] = a
        args.append(nc.dram_tensor(f"in_{name}", a.shape, _mybir.dt.from_np(a.dtype), kind="ExternalInput").ap())
    out = nc.dram_tensor("out_rows", inputs["x"].shape, _mybir.dt.float32, kind="ExternalOutput").ap()
    gnn_program(nc, *args, out)
    r = _run(nc, [arrays], core_ids=[0])
    return r.results[0]["out_rows"]
```

```python
def gnn_program(nc, x, src, dst, edge_weight, weight, bias, out):
    import concourse.bass as bass
    from concourse import mybir
    from contextlib import ExitStack

    f32, i32 = mybir.dt.float32, mybir.dt.int32
    ALU = mybir.AluOpType
    ACT = mybir.ActivationFunctionType

    N, D = x.shape
    E = src.shape[0]
    P = 128
    KC = D // P
    BLOCKS = weight.shape[0] // D
    EPS = 1e-5

    RPP = 4
    UROWS = P * RPP
    UNITS = N // UROWS
    TAIL_ROWS = N - UNITS * UROWS
    TAIL_RPP = 2
    TAIL_P = TAIL_ROWS // TAIL_RPP
    assert TAIL_P * TAIL_RPP == TAIL_ROWS and TAIL_P % 16 == 0
    RING = 3
    BODIES = UNITS // RING
    assert BODIES * RING == UNITS

    EPT = P - 1
    G = 4
    TILES = -(-E // EPT)
    TILES += -TILES % (2 * G)
    GROUPS = TILES // G
    FULL = E // EPT
    REST = E - FULL * EPT
    SLOTS = 2 * P
    assert 0 < REST < EPT and P < FULL < SLOTS - 1 and TILES <= SLOTS
    A_START = 3
    A_END = A_START + GROUPS
    B_START = A_END + 2
    B_GROUPS = BODIES - B_START
    TABLE_OPS = 8
    STEPS = TILES // TABLE_OPS
    LISTED = A_START + STEPS
    assert STEPS * TABLE_OPS == TILES and LISTED + STEPS == A_END
    HALF = TABLE_OPS // 2
    MATCHED = TABLE_OPS // G
    MATCHES = G + 1
    KEYED = FULL + 1
    ABSENT = 1 << 23
    CROWS = TILES * P
    CB = 2 * G
    C_BODIES_MAX = TILES // CB
    C_BODIES_MIN = B_GROUPS * G // CB + 1
    assert B_GROUPS * G % CB == 0
    FIELDS = 4

    v_dram = nc.dram_tensor("v_rows", (CROWS, D), f32).ap()
    list_dram = nc.dram_tensor("packed_edges", (TILES * P, FIELDS), f32).ap()
    c2_list_dram = nc.dram_tensor("c2_list_rows", (CROWS, D), f32).ap()
    keys_out2_dram = nc.dram_tensor("keys_out2", (SLOTS * P,), f32).ap()
    c_dram = [nc.dram_tensor(f"c{n}_rows", (CROWS, D), f32).ap() for n in (1, 2)]
    tail_keys_dram = nc.dram_tensor("tail_keys", (SLOTS, P), f32).ap()
    keys_out_dram = nc.dram_tensor("keys_out", (SLOTS * P,), f32).ap()

    ctx = ExitStack()
    with ctx:
        def sb(name, shape, dt=f32):
            return ctx.enter_context(nc.sbuf_tensor(name, shape, dt))

        def pb(name):
            return ctx.enter_context(nc.psum_tensor(name, [P, 2 * D], f32))

        def sem(name):
            return ctx.enter_context(nc.semaphore(name))

        def sems(name, n):
            return [sem(f"{name}{k}") for k in range(n)]

        ident = sb("ident", [P, P])
        w_sb = sb("w_sb", [P, BLOCKS * KC, D])
        bias4 = sb("bias4", [P, RPP * D])
        bias2 = bias4[:, 0:2 * D]
        ones = sb("ones", [P, P])
        below = sb("below", [P, P])
        below_tile = sb("below_tile", [P, 2, SLOTS])
        eps = sb("eps", [P, 1])
        x_ring = [sb(f"x_ring{k}", [P, RPP * D]) for k in range(RING)]
        xT = [sb(f"xT{k}", [P, 2 * D]) for k in range(2)]
        y_ring = [sb(f"y_ring{k}", [P, RPP * D]) for k in range(RING)]
        o_ring = [sb(f"o_ring{k}", [P, RPP * D]) for k in range(RING)]
        stats = [sb(f"stats{k}", [P, RPP, 6]) for k in range(RING)]
        mean_var = [sb(f"mean_var{k}", [P, RPP, 2]) for k in range(RING)]
        std = [sb(f"std{k}", [P, RPP]) for k in range(RING)]
        rstd = [sb(f"rstd{k}", [P, RPP]) for k in range(RING)]
        shift = [sb(f"shift{k}", [P, RPP]) for k in range(RING)]
        rows_in = [sb(f"rows_in{k}", [P, D]) for k in range(G)]
        ROWS = 2 * G
        sums = [sb(f"sums{k}", [P, G, D]) for k in range(4)]
        sel = [sb(f"sel{k}", [P, P]) for k in range(G)]
        keys_out = sb("keys_out_bc", [P, TILES * P])
        dst_i = sb("dst_i", [P, 2, P], i32)
        next_i = sb("next_i", [P, 2, P], i32)
        src_i = sb("src_i", [P, 2, P], i32)
        w_l = sb("w_l", [P, 2, P])
        dst_f = sb("dst_f", [P, 2, P])
        next_f = sb("next_f", [P, 2, P])
        src_f = sb("src_f", [P, 2, P])
        rows_in += [t[:, :, :].rearrange("p h c -> p (h c)") for t in (w_l, dst_f, next_f, src_f)]
        keys_f = sb("keys_f", [P, 2, P])
        own_r = sb("own_r", [P, 2, P])
        row_r = sb("row_r", [P, 2, P])
        key_in = sb("key_in", [P, SLOTS])
        w1 = sb("w1", [P, SLOTS])
        src_node = sb("src_node", [P, SLOTS], i32)
        tail_node = sb("tail_node", [P, SLOTS], i32)
        tail_f = sb("tail_f", [P, SLOTS])
        src_tail = sb("src_tail", [P, SLOTS], i32)
        own_T = next_i[:, :, :].rearrange("p h c -> p (h c)").bitcast(f32)
        own = sb("own", [P, SLOTS])
        later = sb("later", [1, SLOTS])
        not_padding = sb("not_padding", [P, SLOTS])
        active = sb("active", [P, SLOTS])
        inactive = src_i[:, :, :].rearrange("p h c -> p (h c)").bitcast(f32)
        place_f = dst_i[:, :, :].rearrange("p h c -> p (h c)").bitcast(f32)
        place = sb("place", [P, SLOTS], i32)
        totals = sb("totals", [P, 2])
        totals_bc = sb("totals_bc", [P, 2, P])
        total = sb("total", [1, 1])
        body_starts = sb("body_starts", [1, C_BODIES_MAX])
        started = sb("started", [1, C_BODIES_MAX])
        bodies_f = sb("bodies_f", [1, 1])
        more_bodies = sb("more_bodies", [1, 1], i32)
        packed = sums[1][:, :, :].rearrange("p g d -> p (g d)").rearrange(
            "p (h c f) -> p h c f", h=2, f=FIELDS)
        packed_next = sb("packed_next", [P, 2])
        key_in2 = sb("key_in2", [P, SLOTS])
        w_packed = sb("w_packed", [P, SLOTS])
        src_tail2 = sb("src_tail2", [P, SLOTS], i32)
        own2 = sb("own2", [P, SLOTS], i32)
        record = sb("record", [P, TABLE_OPS, FIELDS])
        gather_idx = [sb(f"gather_idx{k}", [P, G], i32) for k in range(2)]
        tailx_idx = [sb(f"tailx_idx{k}", [P, G], i32) for k in range(2)]
        tailo_idx = [sb(f"tailo_idx{k}", [P, G], i32) for k in range(2)]
        table_idx = sb("table_idx", [P, TABLE_OPS], i32)
        signs = dst_i[:, :, :].rearrange("p h c -> p (h c)").bitcast(f32)
        place_found = sb("place_found", [P, TABLE_OPS])
        tile_row = sb("tile_row", [P, TABLE_OPS])
        row_f = sb("row_f", [P, TABLE_OPS])
        missing = sb("missing", [P, TABLE_OPS])
        source_key = sb("source_key", [P, SLOTS])
        list_blank = sums[2][:, :, :].rearrange("p g d -> p (g d)")[:, 0:TILES * FIELDS]
        zeros = sums[2][:, :, :].rearrange("p g d -> p (g d)")
        tails_found = sums[1][:, :, :].rearrange("p g d -> p (g d)").rearrange("p (k c) -> p k c", c=P)
        spare = sums[3][:, :, :].rearrange("p g d -> p (g d)")
        first_keys = spare[:, 0:KEYED]
        place_number = spare[:, SLOTS:SLOTS + P]
        first_row = spare[:, SLOTS + P:2 * SLOTS]
        bf16 = mybir.dt.bfloat16
        sign_out = [spare[:, 2 * SLOTS:].bitcast(bf16)[:, k * KEYED:(k + 1) * KEYED] for k in range(5)]
        sign_out += [src_tail2[:, :].bitcast(bf16)[:, k * KEYED:(k + 1) * KEYED] for k in range(2)]
        sign_out += [own2[:, :].bitcast(bf16)[:, 0:KEYED]]
        match_out = [t[:, :].bitcast(bf16)[:, k * P:(k + 1) * P] for t in (key_in2, w_packed) for k in range(4)]
        tail_keys = src_i[:, :, :].rearrange("p h c -> p (h c)").bitcast(f32).rearrange("p (h c) -> p h c", c=P)
        own_c2 = [o_ring[1][:, k * D:(k + 1) * D] for k in range(G)]
        v_out = [o_ring[2][:, k * D:(k + 1) * D] for k in range(G)]
        tail_x = [x_ring[0][:, k * D:(k + 1) * D] for k in range(G)]
        c1_in = [x_ring[1][:, k * D:(k + 1) * D] for k in range(G)]
        v_in = [x_ring[2][:, k * D:(k + 1) * D] for k in range(G)]
        cy = [y_ring[2][:, k * D:(k + 1) * D] for k in range(G)]
        co = [o_ring[0][:, k * D:(k + 1) * D] for k in range(G)]
        cstats = [sb(f"cstats{k}", [P, 6]) for k in range(G)]
        cmv = [sb(f"cmv{k}", [P, 2]) for k in range(G)]
        cstd = [sb(f"cstd{k}", [P, 1]) for k in range(G)]
        crstd = [sb(f"crstd{k}", [P, 1]) for k in range(G)]
        cshift = [sb(f"cshift{k}", [P, 1]) for k in range(G)]

        ps_xT = [pb(f"ps_xT{k}") for k in range(2)]
        ps_y = [pb(f"ps_y{k}") for k in range(2)]
        ps_sum = [pb(f"ps_sum{k}") for k in range(2)]
        ps_list = [pb(f"ps_list{k}") for k in range(2)]

        blank = sem("blank")
        consts = sem("consts")
        edges_loaded = sem("edges_loaded")
        weights_loaded = sem("weights_loaded")
        identity_ready = sem("identity_ready")
        w0_ready = sem("w0_ready")
        floats_ready = sem("floats_ready")
        keys_stored = sem("keys_stored")
        keys_loaded = sem("keys_loaded")
        lists_turned = sem("lists_turned")
        table_chain = sem("table_chain")
        tables_ready = sem("tables_ready")
        numbers_ready = sem("numbers_ready")
        table_blank = sem("table_blank")
        x_loaded = sems("x_loaded", RING)
        xT_psum = sem("xT_psum")
        xT_copied = sem("xT_copied")
        y_psum = sem("y_psum")
        y_copied = sem("y_copied")
        stats_ready = sem("stats_ready")
        var_ready = sem("var_ready")
        std_ready = sem("std_ready")
        rstd_ready = sem("rstd_ready")
        shift_ready = sem("shift_ready")
        normed = sem("normed")
        stored = sems("stored", RING)
        gather_staged = sem("gather_staged")
        gathered = sems("gathered", ROWS)
        sel_ready = sem("sel_ready")
        carry_ready = sem("carry_ready")
        summed = sem("summed")
        sum_copied = sem("sum_copied")
        halves_stored = sems("halves_stored", 2)
        c2_scattered = sems("c2_scattered", G)
        c2_idx_staged = sem("c2_idx_staged")
        zeros_ready = sem("zeros_ready")
        c2_blank = sem("c2_blank")
        table_staged = sem("table_staged")
        table_done = sems("table_done", 2)
        found_rows = sem("found_rows")
        matched = sem("matched")
        look_up_chain = sem("look_up_chain")
        firsts_spread = sem("firsts_spread")
        tail_keys_ready = sem("tail_keys_ready")
        tail_keys_stored = sem("tail_keys_stored")
        signs_ready = sem("signs_ready")
        v_blank = sem("v_blank")
        own_chain = sem("own_chain")
        own_turned = sem("own_turned")
        later_ready = sem("later_ready")
        later_spread = sem("later_spread")
        active_ready = sem("active_ready")
        counted = sem("counted")
        totals_ready = sem("totals_ready")
        based = sem("based")
        place_chain = sem("place_chain")
        bodies_ready = sem("bodies_ready")
        packed_blank = sem("packed_blank")
        packed_loaded = sem("packed_loaded")
        packed_floats = sem("packed_floats")
        packed_turned = sem("packed_turned")
        packed_tables = sem("packed_tables")
        keys2_stored = sem("keys2_stored")
        keys2_loaded = sem("keys2_loaded")
        v_staged = sem("v_staged")
        own_loaded = sems("own_loaded", G)
        t_psum = sem("t_psum")
        t_copied = sem("t_copied")
        v_psum = sem("v_psum")
        v_copied = sem("v_copied")
        v_scattered = sems("v_scattered", G)
        tailx_staged = sem("tailx_staged")
        tailo_staged = sem("tailo_staged")
        tailx_in = sems("tailx_in", G)
        c1_loaded = sems("c1_loaded", G)
        v_loaded = sems("v_loaded", G)
        ta_psum = sem("ta_psum")
        ta_copied = sem("ta_copied")
        cy_psum = sem("cy_psum")
        cy_copied = sem("cy_copied")
        cstats_ready = sem("cstats_ready")
        cvar_ready = sem("cvar_ready")
        cstd_ready = sem("cstd_ready")
        crstd_ready = sem("crstd_ready")
        cshift_ready = sem("cshift_ready")
        cnormed = sem("cnormed")
        scattered = sems("scattered", G)

        ctx.enter_context(nc.allow_non_contiguous_dma(reason="a few hundred single keys and four-byte table entries"))
        block = ctx.enter_context(nc.Block())

        def until(eng, s, value):
            if not isinstance(value, int) or value > 0:
                eng.wait_ge(s, value)

        def body_count(eng):
            eng.wait_ge(bodies_ready, 1)
            return eng.value_load(more_bodies[0:1, 0:1], min_val=0, max_val=C_BODIES_MAX - C_BODIES_MIN) + C_BODIES_MIN

        def phase_c_tiles(n_bodies):
            return TILES + CB * n_bodies

        PAIRS = 2 * UNITS + 1

        def unit_rows(ap, u):
            return ap[bass.ds(u * UROWS, UROWS), :].rearrange("(p r) d -> p (r d)", r=RPP)

        tail_rows = [ap[UNITS * UROWS:N, :].rearrange("(p r) d -> p (r d)", r=TAIL_RPP) for ap in (x, out)]

        @block.sync
        def _(sp):
            def as_column(ap):
                return ap.rearrange("(t o) -> t o", o=1)

            sp.dma_start(x_ring[0][:, :], unit_rows(x, 0)).then_inc(x_loaded[0], 16)
            sp.dma_start(w_sb[:, :, :], weight.rearrange("(c p) n -> p c n", p=P)).then_inc(weights_loaded, 16)
            for k in range(RPP):
                sp.dma_start(bias4[:, k * D:(k + 1) * D], bias.partition_broadcast(P)).then_inc(weights_loaded, 16)
            for u in range(1, RING):
                sp.dma_start(x_ring[u][:, :], unit_rows(x, u)).then_inc(x_loaded[u], 16)
            sp.wait_ge(blank, 5)
            for table, ap in ((dst_i, dst), (src_i, src), (w_l, edge_weight)):
                whole = ap[0:FULL * EPT].rearrange("(t c) -> t c", c=EPT)
                sp.dma_start(table[:, 0, 1:P], whole[0:P, :]).then_inc(edges_loaded, 16)
                sp.dma_start(table[0:FULL - P, 1, 1:P], whole[P:FULL, :]).then_inc(edges_loaded, 16)
                sp.dma_start(table[FULL - P:FULL - P + 1, 1, 1:1 + REST],
                             ap[FULL * EPT:E].rearrange("(o c) -> o c", o=1)).then_inc(edges_loaded, 16)
            whole = dst[0:FULL * EPT].rearrange("(t c) -> t c", c=EPT)
            sp.dma_start(dst_i[1:P, 0, 0:1], whole[0:P - 1, EPT - 1:EPT]).then_inc(edges_loaded, 16)
            sp.dma_start(dst_i[0:FULL - P + 1, 1, 0:1], whole[P - 1:FULL, EPT - 1:EPT]).then_inc(edges_loaded, 16)
            sp.dma_start(next_i[:, 0, 0:EPT], whole[0:P, :]).then_inc(edges_loaded, 16)
            sp.dma_start(next_i[0:FULL - P, 1, 0:EPT], whole[P:FULL, :]).then_inc(edges_loaded, 16)
            sp.dma_start(next_i[FULL - P:FULL - P + 1, 1, 0:REST],
                         dst[FULL * EPT:E].rearrange("(o c) -> o c", o=1)).then_inc(edges_loaded, 16)
            sp.dma_start(next_i[:, 0, EPT:P], whole[1:P + 1, 0:1]).then_inc(edges_loaded, 16)
            sp.dma_start(next_i[0:FULL - P - 1, 1, EPT:P], whole[P + 1:FULL, 0:1]).then_inc(edges_loaded, 16)
            sp.dma_start(next_i[FULL - P - 1:FULL - P, 1, EPT:P],
                         as_column(dst[FULL * EPT:FULL * EPT + 1])).then_inc(edges_loaded, 16)
            sp.dma_start(list_dram.rearrange("(p c) f -> p (c f)", p=P), list_blank).then_inc(table_blank, 16)
            def load_unit(u, k):
                sp.wait_ge(xT_psum, 2 * u + 2)
                sp.dma_start(x_ring[k][:, :], unit_rows(x, u + RING)).then_inc(x_loaded[k], 16)

            def store_unit(u, k):
                sp.wait_ge(normed, u + 1)
                sp.dma_start(unit_rows(out, u), o_ring[k][:, :]).then_inc(stored[k], 16)

            def store_half(g, half, table=c_dram[0], before=0):
                sp.wait_ge(sum_copied, G * g + G * before + 2 * half + 2)
                sp.dma_start(table[bass.ds(g * (G * P) + 2 * half * P, 2 * P), :].rearrange("(k p) d -> p k d", p=P),
                             sums[0][:, 2 * half:2 * half + 2, :]).then_inc(halves_stored[half], 16)

            def blank_v(g):
                sp.dma_start(v_dram[bass.ds(g * (G * P), G * P), :].rearrange("(p r) d -> p (r d)", r=G),
                             bias4[:, :]).then_inc(v_blank, 16)
                sp.dma_start(c_dram[1][bass.ds(g * (G * P), G * P), :].rearrange("(p r) d -> p (r d)", r=G),
                             zeros).then_inc(c2_blank, 16)

            def load_keys(g):
                until(sp, keys_loaded, 16 * g)
                sp.dma_start(keys_out[:, bass.ds(g * (G * P), G * P)],
                             keys_out_dram[bass.ds(g * (G * P), G * P)].partition_broadcast(P)).then_inc(keys_loaded, 16)

            def dense_unit(i, k):
                u = RING * i + k
                load_unit(u, k)
                if not isinstance(u, int) or u >= RING:
                    store_unit(u - RING, k)

            for k in range(RING):
                dense_unit(0, k)
            sp.wait_ge(floats_ready, 4)
            sp.dma_start(keys_out_dram.rearrange("(h p c) -> p h c", h=2, c=P), keys_f[:, :, :]).then_inc(keys_stored, 16)
            for k in range(RING):
                dense_unit(1, k)
            sp.wait_ge(tail_keys_ready, 1)
            sp.dma_start(tail_keys_dram.rearrange("(h p) c -> p h c", h=2), tail_keys).then_inc(tail_keys_stored, 16)
            sp.wait_ge(keys_stored, 16)
            load_keys(0)
            with sp.Fori(2, A_START) as i:
                for k in range(RING):
                    dense_unit(i, k)

            def body_a(i, last):
                g = i - A_START
                for k in range(RING):
                    dense_unit(i, k)
                    if k == 0 and not last:
                        load_keys(g + 1)
                    if k == 1:
                        blank_v(g)
                        store_half(g, 0)
                store_half(g, 1)

            sp.wait_ge(zeros_ready, 1)
            with sp.Fori(A_START, A_END - 1) as i:
                body_a(i, False)
            body_a(A_END - 1, True)

            def load_keys2(g):
                until(sp, keys2_loaded, 16 * g)
                sp.dma_start(keys_out[:, bass.ds(g * (G * P), G * P)],
                             keys_out2_dram[bass.ds(g * (G * P), G * P)].partition_broadcast(P)).then_inc(keys2_loaded, 16)

            dense_unit(A_END, 0)
            for half in range(2):
                sp.wait_ge(table_done[half], 16 * HALF * 2 * STEPS)
            sp.wait_ge(packed_blank, 1)
            rows = list_dram[0:TILES * EPT, :].rearrange("(t c) f -> t c f", c=EPT)
            sp.dma_start(packed[:, 0, 1:P, :], rows[0:P, :, :]).then_inc(packed_loaded, 16)
            sp.dma_start(packed[0:TILES - P, 1, 1:P, :], rows[P:TILES, :, :]).then_inc(packed_loaded, 16)
            sp.dma_start(packed[1:P, 0, 0, 0:1], rows[0:P - 1, EPT - 1, 0:1]).then_inc(packed_loaded, 16)
            sp.dma_start(packed[0:TILES - P, 1, 0, 0:1], rows[P - 1:TILES - 1, EPT - 1, 0:1]).then_inc(packed_loaded, 16)
            sp.dma_start(packed_next[:, 0:1], rows[1:P + 1, 0, 0:1]).then_inc(packed_loaded, 16)
            sp.dma_start(packed_next[0:TILES - P - 1, 1:2], rows[P + 1:TILES, 0, 0:1]).then_inc(packed_loaded, 16)
            for k in range(1, RING):
                dense_unit(A_END, k)
            dense_unit(A_END + 1, 0)
            sp.wait_ge(packed_floats, 1)
            sp.dma_start(keys_out2_dram.rearrange("(h p c) -> p h c", h=2, c=P), keys_f[:, :, :]).then_inc(keys2_stored, 16)
            dense_unit(A_END + 1, 1)
            sp.wait_ge(keys2_stored, 16)
            sp.wait_ge(sel_ready, TILES)
            load_keys2(0)
            dense_unit(A_END + 1, 2)

            def body_b(i, last):
                g = i - B_START
                for k in range(RING):
                    u = RING * i + k
                    if not last:
                        load_unit(u, k)
                    elif k == 0:
                        sp.wait_ge(xT_psum, 2 * u + 2)
                        sp.dma_start(x_ring[0][0:TAIL_P, 0:TAIL_RPP * D], tail_rows[0]).then_inc(x_loaded[0], 16)
                    store_unit(u - RING, k)
                    if k == 0:
                        load_keys2(g + 1)
                    if k == 1:
                        store_half(g, 0, c2_list_dram, GROUPS)
                store_half(g, 1, c2_list_dram, GROUPS)

            with sp.Fori(B_START, BODIES - 1) as i:
                body_b(i, False)
            body_b(BODIES - 1, True)
            for u in range(UNITS - RING, UNITS):
                store_unit(u, u % RING)
            sp.wait_ge(normed, UNITS + 1)
            sp.dma_start(tail_rows[1], o_ring[0][0:TAIL_P, 0:TAIL_RPP * D]).then_inc(stored[0], 16)
            n_bodies = body_count(sp)
            with sp.Fori(B_GROUPS, 2 * n_bodies - 1) as g:
                load_keys2(g + 1)
                for half in range(2):
                    store_half(g, half, c2_list_dram, GROUPS)
            for half in range(2):
                store_half(2 * n_bodies - 1, half, c2_list_dram, GROUPS)

            for half in range(2):
                sp.wait_ge(halves_stored[half], n_bodies * 32 + 16 * GROUPS)

            def body_c(j):
                for k in range(CB):
                    n = CB * j + k
                    until(sp, t_psum, n - G + 1)
                    sp.dma_start(own_c2[k % G], c2_list_dram[bass.ds(n * P, P), :]).then_inc(own_loaded[k % G], 16)

            body_c(0)
            with sp.Fori(1, n_bodies) as j:
                body_c(j)

            for k in range(G):
                sp.wait_ge(v_scattered[k], n_bodies * (16 * CB // G))

            def body_d(j):
                for k in range(CB):
                    n = CB * j + k
                    until(sp, ta_psum, n - G + 1)
                    sp.dma_start(c1_in[k % G], c_dram[0][bass.ds(n * P, P), :]).then_inc(c1_loaded[k % G], 16)
                    until(sp, cy_copied, n - G + 1)
                    sp.dma_start(v_in[k % G], v_dram[bass.ds(n * P, P), :]).then_inc(v_loaded[k % G], 16)

            body_d(0)
            with sp.Fori(1, TILES // CB) as j:
                body_d(j)
            for k in range(RING):
                sp.wait_ge(stored[k], 16 * (BODIES + (k == 0)))
            for k in range(G):
                sp.wait_ge(scattered[k], 16 * GROUPS)

        @block.gpsimd
        def _(pool):
            pool.memset(ident[:, :], 0.0).then_inc(consts, 1)
            pool.wait_ge(consts, 1)
            pool.affine_select(out=ident[:, :], in_=ident[:, :], compare_op=ALU.not_equal, fill=1.0,
                               base=0, pattern=[[-1, P]], channel_multiplier=1).then_inc(identity_ready, 1)
            pool.iota(place_number, [[1, P]], base=0, channel_multiplier=0,
                      allow_small_or_imprecise_dtypes=True).then_inc(numbers_ready, 1)
            pool.iota(row_r[:, :, :], [[P * P, 2], [1, P]], base=0, channel_multiplier=P,
                      allow_small_or_imprecise_dtypes=True).then_inc(numbers_ready, 1)
            pool.iota(body_starts[:, :], [[CB * EPT, C_BODIES_MAX]], base=0, channel_multiplier=0,
                      allow_small_or_imprecise_dtypes=True).then_inc(numbers_ready, 1)
            pool.memset(ones[:, :], 1.0).then_inc(consts, 1)
            pool.memset(below[:, :], 1.0).then_inc(consts, 1)
            pool.memset(below_tile[:, :, :], 1.0).then_inc(consts, 1)
            pool.wait_ge(consts, 4)
            pool.affine_select(out=below[:, :], in_=below[:, :], compare_op=ALU.is_gt, fill=0.0,
                               base=0, pattern=[[1, P]], channel_multiplier=-1).then_inc(numbers_ready, 1)
            pool.affine_select(out=below_tile[:, :, :], in_=below_tile[:, :, :], compare_op=ALU.is_gt, fill=0.0,
                               base=0, pattern=[[-P, 2], [1, SLOTS]], channel_multiplier=-1).then_inc(numbers_ready, 1)
            nought = pool.alloc_register("nought")
            bound = pool.alloc_register("bound")
            pool.reg_mov(nought, 0)

            def limit(rows):
                pool.reg_add(bound, nought, rows - 1)

            def gather(dest, table, rows, index, s):
                pool.indirect_dma_start(dest, None, table, bass.IndirectOffsetOnAxis(ap=index, axis=0),
                                        bounds_check=bound, oob_is_err=False).then_inc(s, 16)

            def scatter(table, source, index, s):
                pool.indirect_dma_start(table, bass.IndirectOffsetOnAxis(ap=index, axis=0), source, None,
                                        bounds_check=bound, oob_is_err=False).then_inc(s, 16)

            def gather_a(g, k):
                pool.wait_ge(gather_staged, G * g + k + 1)
                limit(N)
                if not isinstance(g, int) or g > 0:
                    pool.wait_ge(summed, G * g - G + k + 1)
                    limit(N)
                gather(rows_in[k][:, :], x[:, :], N, gather_idx[0][:, k:k + 1], gathered[k])

            def gather_b(g, k):
                pool.wait_ge(gather_staged, G * g + (TILES + k + 1))
                limit(CROWS)
                pool.wait_ge(summed, G * g + (TILES - G + k + 1))
                limit(CROWS)
                gather(rows_in[k][:, :], c_dram[0][:, :], CROWS, gather_idx[0][:, k:k + 1], gathered[k])

            def scatter_c2(g, k):
                pool.wait_ge(c2_idx_staged, G * g + k + 1)
                limit(CROWS)
                pool.wait_ge(sum_copied, G * g + (TILES + k + 1))
                limit(CROWS)
                scatter(c_dram[1][:, :], sums[0][:, k, :], tailo_idx[0][:, k:k + 1], c2_scattered[k])

            def group_b(g, last=False):
                for k in range(G):
                    if not last:
                        gather_b(g + 1, k)
                    if k:
                        scatter_c2(g, k - 1)
                scatter_c2(g, G - 1)

            def table_ops(i, step, ops):
                for k in ops:
                    if k % HALF == 0:
                        pool.wait_ge(table_staged, 2 * (i - A_START) + k // HALF + 1)
                        limit(SLOTS if step == "look up" else TILES * EPT)
                    if k % MATCHED == 0:
                        if step == "look up":
                            until(pool, matched, MATCHES * (i - A_START - 1) + k // MATCHED + 1)
                        limit(SLOTS if step == "look up" else TILES * EPT)
                    if step == "look up":
                        gather(tails_found[:, k, :], tail_keys_dram, SLOTS, table_idx[:, k:k + 1], table_done[k // HALF])
                    else:
                        scatter(list_dram[0:TILES * EPT, :], record[:, k, :], table_idx[:, k:k + 1],
                                table_done[k // HALF])

            def body_a(i, step):
                for k in range(G):
                    table_ops(i, step, range(MATCHED * k, MATCHED * k + MATCHED))
                    if step != "pack, last":
                        gather_a(i - A_START + 1, k)

            pool.wait_ge(blank, 6)
            for k in range(G):
                gather_a(0, k)
            pool.wait_ge(table_blank, 16)
            pool.wait_ge(tail_keys_stored, 16)
            body_a(A_START, "look up")
            with pool.Fori(A_START + 1, LISTED) as i:
                body_a(i, "look up")
            with pool.Fori(LISTED, A_END - 1) as i:
                body_a(i, "pack")
            body_a(A_END - 1, "pack, last")
            for half in range(2):
                pool.wait_ge(halves_stored[half], 16 * GROUPS)
                limit(CROWS)

            pool.wait_ge(c2_blank, 16 * GROUPS)
            limit(CROWS)
            for k in range(G):
                gather_b(0, k)
            group_b(0)
            with pool.Fori(1, B_GROUPS) as g:
                group_b(g)
            n_bodies = body_count(pool)
            with pool.Fori(B_GROUPS, 2 * n_bodies - 1) as g:
                group_b(g)
            group_b(2 * n_bodies - 1, True)

            for half in range(2):
                pool.wait_ge(halves_stored[half], n_bodies * 32 + 16 * GROUPS)
            for k in range(G):
                pool.wait_ge(c2_scattered[k], n_bodies * 32)
            pool.wait_ge(v_blank, 16 * GROUPS)
            pool.wait_ge(normed, UNITS + 1)
            for k in range(RING):
                pool.wait_ge(stored[k], 16 * (BODIES + (k == 0)))
            C_TILES = phase_c_tiles(n_bodies)
            LAG = 6

            def scatter_v(n, group, late):
                pool.wait_ge(v_copied, n + 1)
                limit(CROWS)
                pool.wait_ge(v_staged, group + 1)
                limit(CROWS)
                scatter(v_dram[:, :], v_out[late % G], tailo_idx[late // G][:, late % G:late % G + 1],
                        v_scattered[late % G])

            def body_c(j):
                for k in range(CB):
                    n = CB * j + k
                    if k % G == 0:
                        pool.wait_ge(gather_staged, C_TILES + (G + k // G + 1) + 2 * j)
                        limit(CROWS)
                    pool.wait_ge(summed, C_TILES + (k - ROWS + 1) + CB * j)
                    limit(CROWS)
                    gather(rows_in[k][:, :], c_dram[1][:, :], CROWS, gather_idx[k // G][:, k % G:k % G + 1],
                           gathered[k])
                    if not isinstance(j, int) or k >= LAG:
                        scatter_v(n - LAG, 2 * j + (k - LAG) // G, (k - LAG) % CB)

            body_c(0)
            with pool.Fori(1, n_bodies) as j:
                body_c(j)
            for k in range(CB - LAG, CB):
                scatter_v(CB * n_bodies - CB + k, 2 * n_bodies - 2 + k // G, k)

            def scatter_out(n, group, late):
                pool.wait_ge(cnormed, n + 1)
                limit(N)
                pool.wait_ge(tailo_staged, group + 1)
                limit(N)
                scatter(out[:, :], co[late % G], tailo_idx[late // G][:, late % G:late % G + 1], scattered[late % G])

            def body_d(j):
                for k in range(CB):
                    n = CB * j + k
                    if k % G == 0:
                        pool.wait_ge(tailx_staged, 2 * j + k // G + 1)
                        limit(N)
                    until(pool, ta_psum, n - G + 1)
                    limit(N)
                    gather(tail_x[k % G], x[:, :], N, tailx_idx[k // G][:, k % G:k % G + 1], tailx_in[k % G])
                    if not isinstance(j, int) or k >= LAG:
                        scatter_out(n - LAG, 2 * j + (k - LAG) // G, (k - LAG) % CB)

            body_d(0)
            with pool.Fori(1, TILES // CB) as j:
                body_d(j)
            for n in range(TILES - LAG, TILES):
                scatter_out(n, n // G, n % CB)

        @block.scalar
        def _(act):
            def copy_xT(p, k, rows=P):
                act.wait_ge(xT_psum, p + 1)
                until(act, y_psum, p - 1)
                view = [t[:, :].rearrange("p (q c) -> p q c", c=P)[:, :, 0:rows] for t in (xT[k % 2], ps_xT[k % 2])]
                act.copy(view[0], view[1]).then_inc(xT_copied, 1)

            def roots(u, slot, rows=P, tiles=RPP):
                act.wait_ge(var_ready, u + 1)
                act.activation(std[slot][0:rows, 0:tiles], mean_var[slot][0:rows, 0:tiles, 1], ACT.Sqrt,
                               bias=eps[0:rows, :]).then_inc(std_ready, 1)

            def normalise(u, slot, turn, half, rows=P):
                if half == 0:
                    act.wait_ge(shift_ready, u + 1)
                    until(act, stored[slot], 16 * turn)
                for r in (2 * half, 2 * half + 1):
                    last = act.activation(o_ring[slot][0:rows, r * D:(r + 1) * D], y_ring[slot][0:rows, r * D:(r + 1) * D],
                                          ACT.Identity, bias=shift[slot][0:rows, r:r + 1],
                                          scale=rstd[slot][0:rows, r:r + 1])
                if half == 1 or rows < P:
                    last.then_inc(normed, 1)

            def await_sum(e, carried):
                if carried:
                    act.wait_ge(carry_ready, e + 2)
                else:
                    act.wait_ge(summed, e + 1)

            def copy_sum(e, k, uses, carried, scatters=None):
                await_sum(e, carried)
                if k % 2 == 0:
                    until(act, halves_stored[k // 2], 16 * uses)
                if scatters is not None:
                    until(act, c2_scattered[k], 16 * scatters)
                act.copy(sums[0][:, k, :], ps_sum[k % 2][:, 0:D]).then_inc(sum_copied, 1)

            def pair(i, k):
                copy_xT(2 * RING * i + k, k % 2)
                unit_steps(i, k)

            def unit_steps(i, k):
                u, slot, half = RING * i + k // 2, k // 2, k % 2
                if half == 0 and (not isinstance(u, int) or u >= 3):
                    normalise(u - 3, slot, i - 1, 1)
                if half == 1 and (not isinstance(u, int) or u >= 1):
                    roots(u - 1, (slot - 1) % RING)
                if half == 1 and (not isinstance(u, int) or u >= 2):
                    normalise(u - 2, (slot - 2) % RING, i - (slot < 2), 0)

            def count_tiles(step, ks):
                for k in ks:
                    last = act.activation(sign_out[k], first_keys, ACT.Sign, scale=-1.0,
                                          bias=source_key[:, bass.ds(TABLE_OPS * step + k, 1)],
                                          accum_out=signs[:, bass.ds(TABLE_OPS * step + k, 1)])
                if ks[-1] == TABLE_OPS - 1:
                    last.then_inc(signs_ready, 1)

            act.wait_ge(blank, 6)
            for i in range(3):
                for k in range(2 * RING):
                    pair(i, k)
            act.wait_ge(tables_ready, 3)
            count_tiles(0, range(TABLE_OPS))

            def body_a(i, look_up, b=False):
                g = i - B_START if b else i - A_START
                e = TILES + G * g if b else G * g
                for k in range(2 * RING):
                    if k == 0 and look_up:
                        act.wait_ge(signs_ready, g + 1)
                    copy_xT(2 * RING * i + k, k % 2)
                    for q in ([k - 3] if k < 2 * RING - 1 else [G - 2, G - 1]) if k > 2 else []:
                        copy_sum(e + q, q, g + GROUPS if b else g, q < G - 1, g if b else None)
                    if k < G and look_up:
                        count_tiles(g + 1, range(MATCHED * k, MATCHED * k + MATCHED))
                    unit_steps(i, k)

            body_a(A_START, True)
            with act.Fori(A_START + 1, LISTED - 1) as i:
                body_a(i, True)
            with act.Fori(LISTED - 1, A_END) as i:
                body_a(i, False)
            for i in range(A_END, B_START):
                for k in range(2 * RING):
                    pair(i, k)

            body_a(B_START, False, True)
            with act.Fori(B_START + 1, BODIES) as i:
                body_a(i, False, True)
            copy_xT(2 * UNITS, 0, TAIL_P)
            normalise(UNITS - 3, 0, BODIES - 1, 1)
            roots(UNITS - 1, 2)
            normalise(UNITS - 2, 1, BODIES - 1, 0)
            normalise(UNITS - 2, 1, BODIES - 1, 1)
            roots(UNITS, 0, TAIL_P, TAIL_RPP)
            normalise(UNITS - 1, 2, BODIES - 1, 0)
            normalise(UNITS - 1, 2, BODIES - 1, 1)
            normalise(UNITS, 0, BODIES, 0, TAIL_P)

            n_bodies = body_count(act)
            with act.Fori(B_GROUPS, 2 * n_bodies) as g:
                for k in range(G):
                    copy_sum(TILES + G * g + k, k, g + GROUPS, k < G - 1, g)

            for half in range(2):
                act.wait_ge(halves_stored[half], n_bodies * 32 + 16 * GROUPS)
            for k in range(G):
                act.wait_ge(c2_scattered[k], n_bodies * 32)
            C_TILES = phase_c_tiles(n_bodies)

            def body_c(j):
                for k in range(CB):
                    n = CB * j + k
                    await_sum(C_TILES + n, k < CB - 1)
                    until(act, t_psum, n - G + 1)
                    act.copy(sums[0][:, k % G, :], ps_sum[k % 2][:, 0:D]).then_inc(sum_copied, 1)
                    act.wait_ge(t_psum, n + 1)
                    until(act, v_psum, n - 1)
                    act.copy(xT[k % 2][:, :], ps_xT[k % 2][:, :]).then_inc(t_copied, 1)

            body_c(0)
            with act.Fori(1, n_bodies) as j:
                body_c(j)

            act.wait_ge(normed, UNITS + 1)
            act.wait_ge(v_psum, n_bodies * CB)

            def c_roots(n, k):
                act.wait_ge(cvar_ready, n + 1)
                act.activation(cstd[k % G][:, :], cmv[k % G][:, 1:2], ACT.Sqrt, bias=eps[:, :]).then_inc(cstd_ready, 1)

            def c_normalise(n, k, turn):
                act.wait_ge(cshift_ready, n + 1)
                until(act, scattered[k % G], 16 * turn)
                act.activation(co[k % G], cy[k % G], ACT.Identity, bias=cshift[k % G][:, :],
                               scale=crstd[k % G][:, :]).then_inc(cnormed, 1)

            def d_tile(n, j, k):
                act.wait_ge(ta_psum, n + 1)
                until(act, cy_psum, n - 1)
                act.copy(xT[k % 2][:, :], ps_xT[k % 2][:, :]).then_inc(ta_copied, 1)
                if not isinstance(n, int) or n >= 2:
                    c_roots(n - 2, (k - 2) % G)
                if not isinstance(n, int) or n >= 3:
                    c_normalise(n - 3, (k - 3) % G, j - (k < 3))

            for n in range(2 * G):
                d_tile(n, n // G, n % G)
            with act.Fori(2, GROUPS) as j:
                for k in range(G):
                    d_tile(G * j + k, j, k)
            c_roots(TILES - 2, (TILES - 2) % G)
            c_normalise(TILES - 3, (TILES - 3) % G, GROUPS - 1)
            c_roots(TILES - 1, (TILES - 1) % G)
            c_normalise(TILES - 2, (TILES - 2) % G, GROUPS - 1)
            c_normalise(TILES - 1, (TILES - 1) % G, GROUPS - 1)

        @block.tensor
        def _(pe):
            pe.wait_ge(identity_ready, 1)
            pe.wait_ge(w0_ready, KC)

            def turn_pair(p, k, i, rows=P):
                slot, half = k // 2, k % 2
                if half == 0:
                    pe.wait_ge(x_loaded[slot], 16 * i + 16)
                until(pe, xT_copied, p - 1)
                for r in range(2):
                    for c in range(KC):
                        at = (2 * half + r) * D + c * P
                        q = r * KC + c
                        last = pe.transpose(ps_xT[half][:, q * P:q * P + rows], x_ring[slot][0:rows, at:at + P],
                                            ident[0:rows, 0:rows])
                return last.then_inc(xT_psum, 1)

            def multiply_part(p, half, q, rows=P):
                if q == 0:
                    pe.wait_ge(xT_copied, p + 1)
                    until(pe, y_copied, p - 1)
                r, c = q // KC, q % KC
                last = pe.matmul(ps_y[half][0:rows, r * D:(r + 1) * D], xT[half][:, q * P:q * P + rows],
                                 w_sb[:, c, :], start=c == 0, stop=c == KC - 1)
                if q == 2 * KC - 1:
                    last.then_inc(y_psum, 1)

            def multiply_pair(p, half, rows=P):
                for q in range(2 * KC):
                    multiply_part(p, half, q, rows)

            def sum_tile(e, k, row):
                pe.wait_ge(sel_ready, e + 1)
                pe.wait_ge(carry_ready, e + 1)
                until(pe, sum_copied, e - 1)
                pe.matmul(ps_sum[k % 2][:, 0:D], sel[k % G][:, :], rows_in[row][:, :],
                          start=True, stop=True).then_inc(summed, 1)

            def body_a(i, tiles, b=False):
                for k in range(2 * RING):
                    p = 2 * RING * i + k
                    turn_pair(p, k, i)
                    if not isinstance(p, int) or p >= 1:
                        multiply_pair(p - 1, (k - 1) % 2)
                    if tiles and k >= 2:
                        e = TILES + G * (i - B_START) if b else G * (i - A_START)
                        sum_tile(e + (k - 2), k - 2, k - 2)

            def turn_lists(lists, done):
                for q, rows in enumerate(lists):
                    for h in range(2):
                        at = (2 * (q % 2) + h) * P
                        last = pe.transpose(ps_list[q // 2][:, at:at + P], rows[h], ident[:, :])
                last.then_inc(done, 1)

            body_a(0, False)
            pe.wait_ge(floats_ready, 4)
            turn_lists([[t[:, h, :] for h in range(2)] for t in (dst_f, next_f, src_f, w_l)], lists_turned)
            body_a(1, False)
            pe.wait_ge(tables_ready, 2)
            pe.matmul(ps_list[1][:, SLOTS:SLOTS + KEYED], first_row[:, :], key_in[:, 0:KEYED],
                      start=True, stop=True).then_inc(firsts_spread, 1)
            turn_lists([[own_r[:, h, :] for h in range(2)]], own_turned)
            pe.wait_ge(later_ready, 1)
            pe.matmul(ps_list[1][:, 0:SLOTS], ones[0:1, :], later[:, :], start=True, stop=True).then_inc(later_spread, 1)
            body_a(2, False)
            body_a(A_START, True)
            with pe.Fori(A_START + 1, LISTED) as i:
                body_a(i, True)
            pe.wait_ge(active_ready, 1)
            pe.matmul(ps_list[0][:, 0:SLOTS], below[:, :], active[:, :], start=True, stop=True)
            for h in range(2):
                last = pe.matmul(ps_list[1][:, h:h + 1], active[:, h * P:(h + 1) * P], ones[:, 0:1], start=True, stop=True)
            last.then_inc(counted, 1)
            pe.wait_ge(totals_ready, 1)
            for h in range(2):
                last = pe.matmul(ps_list[1][:, SLOTS:2 * SLOTS], totals_bc[:, h, :], below_tile[:, h, :],
                                 start=h == 0, stop=h == 1)
            last.then_inc(based, 1)
            with pe.Fori(LISTED, A_END) as i:
                body_a(i, True)
            body_a(A_END, False)
            pe.wait_ge(packed_floats, 3)
            turn_lists([[packed[:, h, :, f] for h in range(2)] for f in range(3)]
                       + [[own_r[:, h, :] for h in range(2)]], packed_turned)
            body_a(A_END + 1, False)
            with pe.Fori(B_START, BODIES) as i:
                body_a(i, True, True)
            turn_pair(2 * UNITS, 0, BODIES, TAIL_P)
            multiply_pair(2 * UNITS - 1, 1)
            multiply_pair(2 * UNITS, 0, rows=TAIL_P)
            n_bodies = body_count(pe)
            with pe.Fori(B_GROUPS, 2 * n_bodies) as g:
                for k in range(G):
                    sum_tile(TILES + G * g + k, k, k)

            C_TILES = phase_c_tiles(n_bodies)
            pe.wait_ge(xT_copied, PAIRS)
            pe.wait_ge(y_copied, PAIRS)

            def turn_rows(banks, rows, done):
                for r, part in enumerate(rows):
                    for c in range(KC):
                        q = r * KC + c
                        last = pe.transpose(banks[:, q * P:(q + 1) * P], part[:, c * P:(c + 1) * P], ident[:, :])
                last.then_inc(done, 1)

            def multiply(k, first, done):
                for q in range(2 * KC):
                    last = pe.matmul(ps_y[k % 2][:, 0:D], xT[k % 2][:, q * P:(q + 1) * P], w_sb[:, first + q, :],
                                     start=q == 0, stop=q == 2 * KC - 1)
                last.then_inc(done, 1)

            def multiply_v(n, k):
                pe.wait_ge(t_copied, n + 1)
                until(pe, v_copied, n - 1)
                multiply(k, 2 * KC, v_psum)

            def body_c(j):
                for k in range(CB):
                    n = CB * j + k
                    sum_tile(C_TILES + n, k, k)
                    if not isinstance(n, int) or n > 0:
                        multiply_v(n - 1, k - 1)
                    pe.wait_ge(own_loaded[k % G], 32 * j + 16 * (k // G) + 16)
                    pe.wait_ge(sum_copied, C_TILES + n + 1)
                    until(pe, t_copied, n - 1)
                    turn_rows(ps_xT[k % 2], (own_c2[k % G], sums[0][:, k % G, :]), t_psum)

            body_c(0)
            with pe.Fori(1, n_bodies) as j:
                body_c(j)
            multiply_v(CB * n_bodies - 1, CB - 1)

            pe.wait_ge(t_copied, CB * n_bodies)
            pe.wait_ge(v_copied, CB * n_bodies)

            def multiply_d(n, k):
                pe.wait_ge(ta_copied, n + 1)
                until(pe, cy_copied, n - 1)
                multiply(k, 0, cy_psum)

            def body_d(j):
                for k in range(G):
                    n = G * j + k
                    pe.wait_ge(tailx_in[k], 16 * j + 16)
                    pe.wait_ge(c1_loaded[k], 16 * j + 16)
                    until(pe, ta_copied, n - 1)
                    turn_rows(ps_xT[k % 2], (tail_x[k], c1_in[k]), ta_psum)
                    if not isinstance(n, int) or n > 0:
                        multiply_d(n - 1, k - 1)

            body_d(0)
            with pe.Fori(1, GROUPS) as j:
                body_d(j)
            multiply_d(TILES - 1, TILES - 1)

        @block.vector
        def _(dve):
            dve.memset(dst_i[:, :, :], -1).then_inc(blank, 1)
            dve.memset(next_i[:, :, :], -1).then_inc(blank, 1)
            dve.memset(src_i[:, :, :], ABSENT).then_inc(blank, 1)
            blank_fields = list_blank.rearrange("p (c f) -> p c f", f=FIELDS)
            for f, value in enumerate((-1.0, 0.0, float(ABSENT), float(ABSENT))):
                last = dve.memset(blank_fields[:, :, f], value)
            last.then_inc(blank, 1)
            dve.memset(w_l[:, :, 1:P], 0.0)
            dve.memset(w_l[:, :, 0:1], 1.0).then_inc(blank, 1)
            dve.memset(src_tail[:, :], ABSENT)
            for k in range(G):
                dve.memset(rows_in[k][:, :], 0.0)
            dve.memset(eps[:, :], EPS).then_inc(blank, 1)
            dve.wait_ge(weights_loaded, 16 * (1 + RPP))
            dve.wait_ge(identity_ready, 1)
            for c in range(KC):
                dve.tensor_tensor(w_sb[:, c, c * P:(c + 1) * P], w_sb[:, c, c * P:(c + 1) * P], ident[:, :],
                                  ALU.add).then_inc(w0_ready, 1)
            def columns(dest, table, t, n):
                return dve.tensor_scalar(dest, table[:, bass.ds(t, n)], 0, None, ALU.add)

            def copy_y(p, u, slot, half, rows=P):
                dve.wait_ge(y_psum, p + 1)
                until(dve, normed, u - RING + 1)
                dve.tensor_tensor(y_ring[slot][0:rows, half * 2 * D:(half + 1) * 2 * D], ps_y[half][0:rows, :],
                                  bias2[0:rows, :], ALU.add).then_inc(y_copied, 1)

            def unit_stats(p, slot, half, rows=P):
                dve.wait_ge(y_copied, p + 1)
                for r in (2 * half, 2 * half + 1):
                    last = dve.bn_stats(stats[slot][0:rows, r, :], y_ring[slot][0:rows, r * D:(r + 1) * D])
                last.then_inc(stats_ready, 1)

            def unit_inverse(u, slot, rows=P, tiles=RPP):
                dve.wait_ge(std_ready, u + 1)
                dve.reciprocal(rstd[slot][0:rows, 0:tiles], std[slot][0:rows, 0:tiles]).then_inc(rstd_ready, 1)

            def unit_variance(slot, rows=P, tiles=RPP):
                for r in range(tiles):
                    last = dve.bn_aggr(mean_var[slot][0:rows, r, :], stats[slot][0:rows, r, :])
                last.then_inc(var_ready, 1)

            def unit_shift(u, slot, rows=P, tiles=RPP):
                dve.wait_ge(rstd_ready, u + 1)
                dve.scalar_tensor_tensor(out=shift[slot][0:rows, 0:tiles], in0=mean_var[slot][0:rows, 0:tiles, 0],
                                         scalar=-1.0, in1=rstd[slot][0:rows, 0:tiles], op0=ALU.mult,
                                         op1=ALU.mult).then_inc(shift_ready, 1)

            def unit_end(u, k):
                dve.wait_ge(stats_ready, 2 * u + 2)
                if not isinstance(u, int) or u >= 1:
                    unit_inverse(u - 1, (k - 1) % RING)
                unit_variance(k)
                if not isinstance(u, int) or u >= 1:
                    unit_shift(u - 1, (k - 1) % RING)

            def select(e, k, t, weights, keys=key_in):
                until(dve, summed, e - G + 1)
                dve.tensor_scalar(sel[k % G][:, :], keys_out[:, bass.ds(t * P, P)], keys[:, bass.ds(t, 1)],
                                  weights[:, bass.ds(t, 1)], ALU.is_equal, ALU.mult).then_inc(sel_ready, 1)

            def carry_of(e, gathers, k, before):
                dve.wait_ge(gathered[k], 16 * gathers + 16)
                if before is None:
                    dve.memset(rows_in[k][0:1, :], 0.0).then_inc(carry_ready, 1)
                elif before == "psum":
                    dve.wait_ge(summed, e)
                    dve.tensor_copy(rows_in[k][0:1, :], ps_sum[(k - 1) % 2][0:1, 0:D]).then_inc(carry_ready, 1)
                else:
                    dve.wait_ge(sum_copied, e)
                    dve.tensor_copy(rows_in[k][0:1, :], sums[0][0:1, G - 1, :]).then_inc(carry_ready, 1)

            def stage_table(i, step, half):
                until(dve, table_done[half], 16 * HALF * i)
                to = slice(HALF * half, HALF * half + HALF)
                if step == "look up":
                    if half == 0:
                        dve.wait_ge(signs_ready, i + 1)
                    t = TABLE_OPS * i + HALF * half
                    dve.tensor_scalar(table_idx[:, to], signs[:, bass.ds(t, HALF)], 0.5, KEYED / 2 - 1, ALU.mult,
                                      ALU.add).then_inc(table_staged, 1)
                else:
                    t = TABLE_OPS * (i - STEPS) + HALF * half
                    for f, table in enumerate((key_in, w1, src_tail, own)):
                        columns(record[:, to, f], table, t, HALF)
                    columns(table_idx[:, to], place, t, HALF).then_inc(table_staged, 1)

            def match_tails(step, part):
                for k in range(MATCHED * part, MATCHED * part + MATCHED):
                    last = dve.scalar_tensor_tensor(out=match_out[k], in0=tails_found[:, k, :],
                                                    scalar=source_key[:, bass.ds(TABLE_OPS * step + k, 1)],
                                                    in1=place_number, op0=ALU.is_equal, op1=ALU.mult,
                                                    accum_out=place_found[:, k:k + 1])
                last.then_inc(matched, 1)

            def rows_found(step):
                cols = bass.ds(TABLE_OPS * step, TABLE_OPS)
                dve.tensor_scalar(tile_row[:, :], signs[:, cols], 0.5 * P, (KEYED / 2 - 1) * P, ALU.mult,
                                  ALU.add).then_inc(matched, 1)
                dve.wait_ge(matched, MATCHES * step + MATCHES)
                dve.tensor_tensor(row_f[:, :], tile_row[:, :], place_found[:, :], ALU.add)
                dve.tensor_scalar(missing[:, :], place_found[:, :], 0.0, float(ABSENT), ALU.is_equal,
                                  ALU.mult).then_inc(look_up_chain, 1)
                dve.wait_ge(look_up_chain, step + 1)
                dve.tensor_tensor(src_tail[:, cols], row_f[:, :], missing[:, :], ALU.add).then_inc(found_rows, 1)

            def copy_pair(i, k):
                copy_y(2 * RING * i + k, RING * i + k // 2, k // 2, k % 2)

            def measure_pair(i, k):
                u, slot, half = RING * i + k // 2, k // 2, k % 2
                unit_stats(2 * RING * i + k, slot, half)
                if half:
                    unit_end(u, slot)

            def dense_body(i, pairs=range(2 * RING)):
                for k in pairs:
                    copy_pair(i, k)
                    measure_pair(i, k)

            def next_index(g, k, last, b=False):
                if not last:
                    columns(gather_idx[0][:, k:k + 1], src_tail2 if b else src_node, G * g + G + k,
                            1).then_inc(gather_staged, 1)
                if b:
                    until(dve, c2_scattered[k], 16 * g)
                    columns(tailo_idx[0][:, k:k + 1], own2, G * g + k, 1).then_inc(c2_idx_staged, 1)

            def body_a(i, step, last=False, before_last_pair=None, b=False):
                g = i - B_START if b else i - A_START
                t = G * g
                e = TILES + G * g if b else G * g
                uses = GROUPS + g if b else g
                weights, keys = (w_packed, key_in2) if b else (w1, key_in)
                found = step == "look up" and not (isinstance(g, int) and g == 0)
                dve.wait_ge(keys2_loaded if b else keys_loaded, 16 * g + 16)
                select(e, 0, t, weights, keys)
                copy_pair(i, 0)
                carry_of(e, uses, 0, None if isinstance(g, int) and g == 0 else "sums")
                next_index(g, 0, last, b)
                measure_pair(i, 0)
                select(e + 1, 1, t + 1, weights, keys)
                for k in range(G):
                    copy_pair(i, k + 1)
                    if k + 1 < G:
                        carry_of(e + k + 1, uses, k + 1, "psum")
                        next_index(g, k + 1, last, b)
                    if k + 2 < G:
                        select(e + k + 2, k + 2, t + k + 2, weights, keys)
                    if k < 2 and not b:
                        stage_table(g, step, k)
                    if found:
                        match_tails(g - 1, k)
                    measure_pair(i, k + 1)
                if found:
                    rows_found(g - 1)
                if before_last_pair is not None:
                    before_last_pair()
                copy_pair(i, G + 1)
                measure_pair(i, G + 1)

            dense_body(0, range(2 * RING - 1))
            dve.wait_ge(edges_loaded, 16 * 17)
            dve.tensor_copy(dst_f[:, :, :], dst_i[:, :, :]).then_inc(floats_ready, 1)
            dve.tensor_copy(next_f[:, :, :], next_i[:, :, :]).then_inc(floats_ready, 1)
            dve.tensor_copy(src_f[:, :, :], src_i[:, :, :]).then_inc(floats_ready, 1)
            dve.tensor_copy(keys_f[:, :, 1:P], dst_i[:, :, 1:P])
            dve.tensor_copy(keys_f[:, :, 0:1], dst_i[:, :, P - 1:P]).then_inc(floats_ready, 1)
            dve.wait_ge(lists_turned, 1)
            dve.tensor_copy(key_in[:, :], ps_list[0][:, 0:SLOTS]).then_inc(table_chain, 1)
            dve.tensor_copy(src_node[:, :], ps_list[1][:, 0:SLOTS])
            dve.tensor_copy(w1[:, :], ps_list[1][:, SLOTS:2 * SLOTS])
            dve.wait_ge(table_chain, 1)
            dve.tensor_tensor(tail_f[:, :], key_in[:, :], ps_list[0][:, SLOTS:2 * SLOTS],
                              ALU.is_equal).then_inc(table_chain, 1)
            dve.wait_ge(table_chain, 2)
            dve.scalar_tensor_tensor(out=tail_node[:, :], in0=tail_f[:, :], scalar=float(ABSENT), in1=key_in[:, :],
                                     op0=ALU.mult, op1=ALU.add).then_inc(table_chain, 1)
            dve.wait_ge(table_chain, 3)
            dve.memset(tail_node[0:1, :], ABSENT)
            dve.wait_ge(consts, 4)
            dve.tensor_scalar(first_row[:, :], ones[:, :], ident[:, 1:2], None, ALU.mult).then_inc(tables_ready, 1)
            dve.tensor_scalar(source_key[:, :], src_node[:, :], 0.5, None, ALU.add)
            dve.tensor_scalar(not_padding[:, :], src_node[:, :], N, None, ALU.is_lt)
            dve.wait_ge(numbers_ready, 5)

            steps_done = [0]

            def after(instruction, s, count):
                count[0] += 1
                instruction.then_inc(s, 1)
                dve.wait_ge(s, count[0])

            after(dve.tensor_tensor(own_r[:, :, :], dst_f[:, :, :], next_f[:, :, :], ALU.is_equal), own_chain, steps_done)
            after(dve.scalar_tensor_tensor(out=tail_keys, in0=own_r[:, :, :], scalar=-float(ABSENT),
                                           in1=dst_f[:, :, :], op0=ALU.mult, op1=ALU.add), own_chain, steps_done)
            dve.tensor_scalar(tail_keys, tail_keys, 0.5, None, ALU.add).then_inc(tail_keys_ready, 1)
            after(dve.scalar_tensor_tensor(out=own_r[:, :, :], in0=own_r[:, :, :], scalar=float(ABSENT),
                                           in1=row_r[:, :, :], op0=ALU.mult, op1=ALU.add), own_chain, steps_done)
            after(dve.memset(own_r[:, :, 0:1], float(ABSENT)), own_chain, steps_done)
            for d in (1, 2, 4, 8, 16, 32, 64):
                after(dve.tensor_tensor(own_r[:, :, 0:P - d], own_r[:, :, 0:P - d], own_r[:, :, d:P], ALU.min),
                      own_chain, steps_done)
            dve.memset(later[:, :], float(ABSENT)).then_inc(tables_ready, 1)
            columns(gather_idx[0][:, :], src_node, 0, G).then_inc(gather_staged, G)
            dense_body(0, range(2 * RING - 1, 2 * RING))
            dense_body(1, range(2 * RING - 1))
            dve.wait_ge(firsts_spread, 1)
            dve.tensor_copy(first_keys[:, 1:KEYED], ps_list[1][:, SLOTS + 1:SLOTS + KEYED])
            dve.memset(first_keys[:, 0:1], -1.0).then_inc(tables_ready, 1)
            dve.wait_ge(own_turned, 1)
            after(dve.tensor_copy(own_T[:, :], ps_list[0][:, 0:SLOTS]), own_chain, steps_done)
            after(dve.tensor_copy(later[:, 0:SLOTS - 1], own_T[0:1, 1:SLOTS]), own_chain, steps_done)
            for d in (1, 2, 4, 8, 16, 32, 64, 128):
                after(dve.tensor_tensor(later[:, 0:SLOTS - d], later[:, 0:SLOTS - d], later[:, d:SLOTS], ALU.min),
                      own_chain, steps_done)
            dve.memset(missing[:, :], 0.0).then_inc(later_ready, 1)
            dve.wait_ge(table_blank, 16)
            dve.memset(zeros, 0.0).then_inc(zeros_ready, 1)
            dve.wait_ge(later_spread, 1)
            after(dve.tensor_tensor(own[:, :], own_T[:, :], ps_list[1][:, 0:SLOTS], ALU.min), own_chain, steps_done)
            dense_body(1, range(2 * RING - 1, 2 * RING))
            dense_body(2)

            def find_places():
                for half in range(2):
                    dve.wait_ge(table_done[half], 16 * HALF * STEPS)
                for part in range(G):
                    match_tails(STEPS - 1, part)
                rows_found(STEPS - 1)
                dve.wait_ge(found_rows, STEPS)
                dve.wait_ge(tail_keys_stored, 16)
                dve.scalar_tensor_tensor(out=active[:, :], in0=src_tail[:, :], scalar=float(CROWS),
                                         in1=not_padding[:, :], op0=ALU.is_lt, op1=ALU.mult).then_inc(active_ready, 1)
                dve.wait_ge(active_ready, 1)
                done = [0]
                after(dve.tensor_scalar(inactive[:, :], active[:, :], -float(ABSENT), float(ABSENT), ALU.mult, ALU.add),
                      place_chain, done)
                dve.wait_ge(counted, 1)
                after(dve.tensor_copy(totals[:, :], ps_list[1][:, 0:2]), place_chain, done)
                for h in range(2):
                    last = dve.tensor_scalar(totals_bc[:, h, :], ones[:, :], totals[:, h:h + 1], None, ALU.mult)
                last.then_inc(totals_ready, 1)
                after(dve.tensor_tensor(place_f[:, :], inactive[:, :], ps_list[0][:, 0:SLOTS], ALU.add), place_chain, done)
                dve.wait_ge(based, 1)
                after(dve.tensor_tensor(place[:, :], place_f[:, :], ps_list[1][:, SLOTS:2 * SLOTS], ALU.add),
                      place_chain, done)
                after(dve.tensor_copy(total[:, :], ps_list[1][0:1, SLOTS + TILES:SLOTS + TILES + 1]), place_chain, done)
                after(dve.tensor_scalar(started[:, :], body_starts[:, :], total[:, :], None, ALU.is_lt), place_chain, done)
                after(dve.reduce_sum(bodies_f[:, :], started[:, :], mybir.AxisListType.X), place_chain, done)
                dve.tensor_scalar(more_bodies[:, :], bodies_f[:, :], -float(C_BODIES_MIN), 0.0, ALU.add, ALU.max).then_inc(bodies_ready, 1)

            body_a(A_START, "look up")
            with dve.Fori(A_START + 1, LISTED - 1) as i:
                body_a(i, "look up")
            body_a(LISTED - 1, "look up", before_last_pair=find_places)
            dve.memset(packed[:, :, 1:P, :], 0.0)
            dve.memset(packed[:, :, 0, 0], -1.0)
            dve.memset(packed[:, :, 0, 1], 1.0)
            dve.memset(packed[:, :, 0, 2:FIELDS], float(ABSENT))
            dve.memset(packed_next[:, :], -1.0).then_inc(packed_blank, 1)
            with dve.Fori(LISTED, A_END - 1) as i:
                body_a(i, "pack")
            body_a(A_END - 1, "pack", last=True)
            dense_body(A_END, range(2 * RING - 1))
            dve.wait_ge(packed_loaded, 16 * 6)
            dve.wait_ge(keys_stored, 16)
            dve.tensor_copy(keys_f[:, :, 1:P], packed[:, :, 1:P, 0])
            dve.tensor_copy(keys_f[:, :, 0:1], packed[:, :, P - 1:P, 0]).then_inc(packed_floats, 1)
            dve.tensor_tensor(own_r[:, :, 0:P - 1], packed[:, :, 0:P - 1, 0], packed[:, :, 1:P, 0], ALU.is_equal)
            after(dve.tensor_tensor(own_r[:, :, P - 1], packed[:, :, P - 1, 0], packed_next[:, :], ALU.is_equal),
                  own_chain, steps_done)
            after(dve.scalar_tensor_tensor(out=own_r[:, :, :], in0=own_r[:, :, :], scalar=float(ABSENT),
                                           in1=packed[:, :, :, 3], op0=ALU.mult, op1=ALU.add), own_chain, steps_done)
            dve.memset(own_r[:, :, 0:1], float(ABSENT)).then_inc(packed_floats, 2)
            dense_body(A_END, range(2 * RING - 1, 2 * RING))
            dense_body(A_END + 1, range(2))
            dve.wait_ge(packed_turned, 1)
            dve.tensor_copy(key_in2[:, :], ps_list[0][:, 0:SLOTS])
            dve.tensor_copy(w_packed[:, :], ps_list[0][:, SLOTS:2 * SLOTS])
            dve.tensor_copy(src_tail2[:, :], ps_list[1][:, 0:SLOTS])
            dve.tensor_copy(own2[:, :], ps_list[1][:, SLOTS:2 * SLOTS]).then_inc(packed_tables, 1)
            dve.wait_ge(packed_tables, 1)

            columns(gather_idx[0][:, :], src_tail2, 0, G).then_inc(gather_staged, G)
            dense_body(A_END + 1, range(2, 2 * RING))
            body_a(B_START, None, b=True)
            with dve.Fori(B_START + 1, BODIES) as i:
                body_a(i, None, b=True)
            copy_y(2 * UNITS, UNITS, 0, 0, TAIL_P)
            unit_stats(2 * UNITS, 0, 0, TAIL_P)
            dve.wait_ge(stats_ready, 2 * UNITS + 1)
            unit_inverse(UNITS - 1, RING - 1)
            unit_variance(0, TAIL_P, TAIL_RPP)
            unit_shift(UNITS - 1, RING - 1)
            unit_inverse(UNITS, 0, TAIL_P, TAIL_RPP)
            unit_shift(UNITS, 0, TAIL_P, TAIL_RPP)
            n_bodies = body_count(dve)
            with dve.Fori(B_GROUPS, 2 * n_bodies) as g:
                t, e, uses = G * g, TILES + G * g, GROUPS + g
                dve.wait_ge(keys2_loaded, 16 * g + 16)
                select(e, 0, t, w_packed, key_in2)
                carry_of(e, uses, 0, "sums")
                next_index(g, 0, False, True)
                select(e + 1, 1, t + 1, w_packed, key_in2)
                for k in range(1, G):
                    carry_of(e + k, uses, k, "psum")
                    next_index(g, k, False, True)
                    if k + 1 < G:
                        select(e + k + 1, k + 1, t + k + 1, w_packed, key_in2)

            C_TILES = phase_c_tiles(n_bodies)
            for k in range(G):
                dve.wait_ge(c2_scattered[k], n_bodies * 32)
            dve.wait_ge(normed, UNITS + 1)
            for k in range(RING):
                dve.wait_ge(stored[k], 16 * (BODIES + (k == 0)))

            def stage_c(g, half):
                columns(gather_idx[half][:, :], src_tail2, G * g, G).then_inc(gather_staged, 1)

            def copy_v(n, k, turn):
                dve.wait_ge(v_psum, n + 1)
                until(dve, v_scattered[k % G], 16 * turn)
                dve.tensor_tensor(v_out[k % G], ps_y[k % 2][:, 0:D], bias4[:, 0:D], ALU.add).then_inc(v_copied, 1)

            def body_c(j):
                select(C_TILES + CB * j, 0, CB * j, w_packed, key_in2)
                carry_of(C_TILES + CB * j, 2 * n_bodies + GROUPS + j, 0, None if isinstance(j, int) and j == 0 else "sums")
                select(C_TILES + CB * j + 1, 1, CB * j + 1, w_packed, key_in2)
                for k in range(CB):
                    n, g = CB * j + k, 2 * j + k // G
                    if k % G == 0:
                        stage_c(g + 1, (k // G + 1) % 2)
                    if k + 1 < CB:
                        carry_of(C_TILES + n + 1, 2 * n_bodies + GROUPS + j if k + 1 < G else j, k + 1, "psum")
                    if k + 2 < CB:
                        select(C_TILES + n + 2, k + 2, n + 2, w_packed, key_in2)
                    if k % G == 1:
                        for q in range(G):
                            until(dve, v_scattered[q], 16 * (g - 1))
                        columns(tailo_idx[k // G][:, :], own2, G * g, G).then_inc(v_staged, 1)
                    if not isinstance(n, int) or n > 0:
                        copy_v(n - 1, k - 1, g - (k % G == 0))

            stage_c(0, 0)
            body_c(0)
            body_c(1)
            with dve.Fori(2, n_bodies) as j:
                body_c(j)
            copy_v(CB * n_bodies - 1, CB - 1, 2 * n_bodies - 1)

            for q in range(G):
                dve.wait_ge(v_scattered[q], n_bodies * (16 * CB // G))

            def stage_d(g, half):
                columns(tailx_idx[half][:, :], tail_node, G * g, G).then_inc(tailx_staged, 1)

            def c_copy(n, k, use):
                dve.wait_ge(cy_psum, n + 1)
                dve.wait_ge(v_loaded[k % G], 16 * use)
                until(dve, cnormed, n - G + 1)
                dve.tensor_tensor(cy[k % G], ps_y[k % 2][:, 0:D], v_in[k % G], ALU.add).then_inc(cy_copied, 1)
                dve.wait_ge(cy_copied, n + 1)
                dve.bn_stats(cstats[k % G][:, :], cy[k % G]).then_inc(cstats_ready, 1)

            def c_inverse(n, k):
                dve.wait_ge(cstd_ready, n + 1)
                dve.reciprocal(crstd[k % G][:, :], cstd[k % G][:, :]).then_inc(crstd_ready, 1)

            def c_variance(k):
                dve.bn_aggr(cmv[k % G][:, :], cstats[k % G][:, :]).then_inc(cvar_ready, 1)

            def c_shift(n, k):
                dve.wait_ge(crstd_ready, n + 1)
                dve.scalar_tensor_tensor(out=cshift[k % G][:, :], in0=cmv[k % G][:, 0:1], scalar=-1.0,
                                         in1=crstd[k % G][:, :], op0=ALU.mult, op1=ALU.mult).then_inc(cshift_ready, 1)

            def c_finish(n, k, use):
                if not isinstance(n, int) or n >= 1:
                    c_copy(n - 1, k - 1, use)
                    dve.wait_ge(cstats_ready, n)
                    if not isinstance(n, int) or n >= 2:
                        c_inverse(n - 2, k - 2)
                    c_variance(k - 1)
                    if not isinstance(n, int) or n >= 2:
                        c_shift(n - 2, k - 2)

            def body_d(j):
                for k in range(CB):
                    n, g = CB * j + k, 2 * j + k // G
                    if k % G == 0:
                        for q in range(G):
                            until(dve, tailx_in[q], 16 * g)
                        stage_d(g + 1, (k // G + 1) % 2)
                    if k % G == 1:
                        for q in range(G):
                            until(dve, scattered[q], 16 * (g - 1))
                        columns(tailo_idx[k // G][:, :], tail_node, G * g, G).then_inc(tailo_staged, 1)
                    c_finish(n, k, g + (k % G > 0))

            stage_d(0, 0)
            body_d(0)
            with dve.Fori(1, TILES // CB) as j:
                body_d(j)
            c_finish(TILES, TILES, GROUPS)
            c_inverse(TILES - 1, TILES - 1)
            c_shift(TILES - 1, TILES - 1)


_INS = ["x", "src", "dst", "edge_weight", "L0_gnn_shared_weight", "L0_gnn_output_bias"]


def kernel(**inputs):
    import numpy as _np
    import concourse.bacc as _bacc
    from concourse import mybir as _mybir
    from concourse.bass_utils import run_bass_kernel_spmd as _run

    nc = _bacc.Bacc("TRN2", target_bir_lowering=False, num_devices=1)
    arrays, args = {}, []
    for name in _INS:
        a = _np.ascontiguousarray(inputs[name])
        arrays[f"in_{name}"] = a
        args.append(nc.dram_tensor(f"in_{name}", a.shape, _mybir.dt.from_np(a.dtype), kind="ExternalInput").ap())
    out = nc.dram_tensor("out_rows", inputs["x"].shape, _mybir.dt.float32, kind="ExternalOutput").ap()
    gnn_program(nc, *args, out)
    r = _run(nc, [arrays], core_ids=[0])
    return r.results[0]["out_rows"]
```
